# Optimizing a Trainium2 kernel written in Bass

```python
import numpy as np
import jax
import jax.numpy as jnp

def _softmax(x, axis=-1):
    return jax.nn.softmax(x, axis=axis)

def _gelu(x):
    return jax.nn.gelu(x, approximate=True)

def _silu(x):
    return jax.nn.silu(x)

def _sigmoid(x):
    return jax.nn.sigmoid(x)

def _layernorm(x, axis=-1, eps=1e-05):
    m = jnp.mean(x, axis=axis, keepdims=True)
    v = jnp.var(x, axis=axis, keepdims=True)
    return (x - m) / jnp.sqrt(v + eps)

def _scatter_add(tgt, idx, src, axis=0):
    return tgt.at[idx].add(src)

def _segment_sum(src, seg, n):
    return jax.ops.segment_sum(src, seg, n)
kernel_name = 'mk_prb_d1_jaxref_r4_cf31a5'

def setup_inputs(seed: int=0):
    np.random.seed(seed)
    _w = jnp.asarray

    def _L0_attn_setup():
        import jax, jax.numpy as jnp
        import numpy as np
        NUM_HEADS = 16
        FOCUS_FACTOR = 1.6
        HEAD_REGION = {0: 0, 1: 1, 2: 2}

        def _region_multipliers(seq_len: int, num_heads: int, factor: float) -> jnp.ndarray:
            first_end = max(1, seq_len // 3)
            second_end = max(first_end + 1, 2 * seq_len // 3)
            pos = jnp.arange(seq_len)
            regions = [pos < first_end, (pos >= first_end) & (pos < second_end), pos >= second_end]
            mult = np.ones((num_heads, seq_len), dtype=np.float32)
            mult = jnp.asarray(mult)
            for h, r in HEAD_REGION.items():
                if h < num_heads:
                    mult = mult.at[h].set(1.0 + (factor - 1.0) * regions[r].astype(jnp.float32))
            return mult
        key = jax.random.key(seed)
        k1, k2, k3, k4, k5 = jax.random.split(key, 5)
        B, S, D = (2, 512, 256)
        return {'hidden_states': jax.random.normal(k1, (B, S, D), dtype=jnp.float32), 'c_attn_w': jax.random.normal(k2, (D, 3 * D), dtype=jnp.float32) * 0.02, 'c_attn_b': jax.random.normal(k3, (3 * D,), dtype=jnp.float32) * 0.02, 'c_proj_w': jax.random.normal(k4, (D, D), dtype=jnp.float32) * 0.02, 'c_proj_b': jax.random.normal(k5, (D,), dtype=jnp.float32) * 0.02}
    _L0_attn_in = _L0_attn_setup()

    def _L0_ffn_setup():
        import jax, jax.numpy as jnp
        import numpy as np
        HID, FFN, E, K = (256, 1024, 8, 2)
        CAP_FACTOR = 1.25
        key = jax.random.key(seed)
        k1, k2, k3, k4 = jax.random.split(key, 4)
        B, T = (4, 512)
        x = jax.random.normal(k1, (B, T, HID), dtype=jnp.float32)
        router_w = jax.random.normal(k2, (E, HID), dtype=jnp.float32) * 0.02
        w1 = jax.random.normal(k3, (E, HID, FFN), dtype=jnp.float32) * 0.02
        w2 = jax.random.normal(k4, (E, FFN, HID), dtype=jnp.float32) * 0.02
        return {'x': x, 'router_w': router_w, 'w1': w1, 'w2': w2}
    _L0_ffn_in = _L0_ffn_setup()
    _d = {'L0_attn_hidden_states': _L0_attn_in['hidden_states'], 'L0_attn_c_attn_w': _L0_attn_in['c_attn_w'], 'L0_attn_c_attn_b': _L0_attn_in['c_attn_b'], 'L0_attn_c_proj_w': _L0_attn_in['c_proj_w'], 'L0_attn_c_proj_b': _L0_attn_in['c_proj_b'], 'L0_ffn_router_w': _L0_ffn_in['router_w'], 'L0_ffn_w1': _L0_ffn_in['w1'], 'L0_ffn_w2': _L0_ffn_in['w2']}
    _x0 = _d['L0_attn_hidden_states']
    _d['L0_attn_hidden_states'] = jax.random.normal(jax.random.fold_in(jax.random.key(seed), 1), (1, 4096, 256), dtype=_x0.dtype)
    del _x0
    return _d

def reference(L0_attn_hidden_states, L0_attn_c_attn_w, L0_attn_c_attn_b, L0_attn_c_proj_w, L0_attn_c_proj_b, L0_ffn_router_w, L0_ffn_w1, L0_ffn_w2):

    def _L0_attn_ref(hidden_states, c_attn_w, c_attn_b, c_proj_w, c_proj_b):
        import jax, jax.numpy as jnp
        import numpy as np
        NUM_HEADS = 16
        FOCUS_FACTOR = 1.6
        HEAD_REGION = {0: 0, 1: 1, 2: 2}

        def _region_multipliers(seq_len: int, num_heads: int, factor: float) -> jnp.ndarray:
            first_end = max(1, seq_len // 3)
            second_end = max(first_end + 1, 2 * seq_len // 3)
            pos = jnp.arange(seq_len)
            regions = [pos < first_end, (pos >= first_end) & (pos < second_end), pos >= second_end]
            mult = np.ones((num_heads, seq_len), dtype=np.float32)
            mult = jnp.asarray(mult)
            for h, r in HEAD_REGION.items():
                if h < num_heads:
                    mult = mult.at[h].set(1.0 + (factor - 1.0) * regions[r].astype(jnp.float32))
            return mult
        B, S, D = hidden_states.shape
        H = NUM_HEADS
        hd = D // H
        qkv = hidden_states @ c_attn_w + c_attn_b
        q, k, v = jnp.split(qkv, 3, axis=-1)

        def _reshape(x):
            return x.reshape(B, S, H, hd).transpose(0, 2, 1, 3)
        q, k, v = (_reshape(q), _reshape(k), _reshape(v))
        scores = jnp.einsum('bhqd,bhkd->bhqk', q, k) / jnp.sqrt(jnp.float32(hd))
        causal = jnp.tril(jnp.ones((S, S), dtype=bool))
        mask_value = jnp.finfo(scores.dtype).min
        scores = jnp.where(causal[None, None], scores, mask_value)
        attn = jax.nn.softmax(scores, axis=-1)
        mult = _region_multipliers(S, H, FOCUS_FACTOR)
        scaled = attn * mult[None, :, None, :]
        scaled = scaled / jnp.sum(scaled, axis=-1, keepdims=True)
        div_heads = jnp.zeros((H,), dtype=bool)
        for h in HEAD_REGION:
            if h < H:
                div_heads = div_heads.at[h].set(True)
        attn = jnp.where(div_heads[None, :, None, None], scaled, attn)
        out = jnp.einsum('bhqk,bhkd->bhqd', attn, v)
        out = out.transpose(0, 2, 1, 3).reshape(B, S, D)
        out = out @ c_proj_w + c_proj_b
        return out

    def _L0_ffn_ref(x, router_w, w1, w2):
        import jax, jax.numpy as jnp
        import numpy as np
        HID, FFN, E, K = (256, 1024, 8, 2)
        CAP_FACTOR = 1.25
        B, T, H = x.shape
        N = B * T
        x_flat = x.reshape(N, H)
        C = max(1, int(CAP_FACTOR * N / E * K))
        logits = x_flat @ router_w.T
        probs = jax.nn.softmax(logits, axis=-1)
        top_v, top_i = jax.lax.top_k(probs, K)
        top_v = top_v / jnp.sum(top_v, axis=-1, keepdims=True)
        out = jnp.zeros_like(x_flat)
        for k in range(K):
            eid = top_i[:, k]
            gate = top_v[:, k]
            onehot = jax.nn.one_hot(eid, E, dtype=jnp.int32)
            pos = jnp.take_along_axis(jnp.cumsum(onehot, axis=0), eid[:, None], axis=1)[:, 0] - 1
            keep = pos < C
            slot = jnp.where(keep, eid * C + pos, E * C)
            buf = jnp.zeros((E * C + 1, H), dtype=x.dtype).at[slot].add(x_flat * keep[:, None].astype(x.dtype))
            expert_in = buf[:E * C].reshape(E, C, H)
            h = jax.nn.gelu(jnp.einsum('ech,ehf->ecf', expert_in, w1), approximate=False)
            y = jnp.einsum('ecf,efh->ech', h, w2)
            tok = y.reshape(E * C, H)[jnp.minimum(slot, E * C - 1)]
            out = out + tok * (gate * keep.astype(x.dtype))[:, None]
        return out.reshape(B, T, H)
    x = L0_attn_hidden_states
    xn = _layernorm(x, axis=-1)
    x = x + _L0_attn_ref(xn, L0_attn_c_attn_w, L0_attn_c_attn_b, L0_attn_c_proj_w, L0_attn_c_proj_b) + _L0_ffn_ref(xn, L0_ffn_router_w, L0_ffn_w1, L0_ffn_w2)
    return x

_drawn_inputs = setup_inputs


def setup_inputs(seed=0):
    import zlib

    import numpy as np

    out = dict(_drawn_inputs(seed))
    spreads = {}
    factors = {'L0_attn_c_attn_w': 8.0,
     'L0_attn_c_attn_b': 7.628,
     'L0_attn_c_proj_w': 6.965,
     'L0_attn_c_proj_b': 12.15,
     'L0_ffn_router_w': 3.443,
     'L0_ffn_w1': 3.074,
     'L0_ffn_w2': 2.993}
    for name, (base, spread) in spreads.items():
        noise = np.random.default_rng([zlib.crc32(name.encode()), seed]).standard_normal(out[name].shape)
        drawn = base * np.exp(spread * noise) if base else spread * noise
        out[name] = jnp.asarray(drawn.astype(out[name].dtype))
    for name, factor in factors.items():
        out[name] = (out[name] * factor).astype(out[name].dtype)
    return out
```

```python
import numpy as np

import concourse.bass as bass
from concourse import mybir

P = 128
F32 = mybir.dt.float32
BF16 = mybir.dt.bfloat16
I32 = mybir.dt.int32
ALU = mybir.AluOpType
ACT = mybir.ActivationFunctionType
AX = mybir.AxisListType.X

S, D, H, HD = 4096, 256, 16, 16
E, F, CAP = 8, 1024, 1280
TOPK = 2
NT = S // P
CH = 512
NCH = S // CH
KD = D // P
KF = F // P
VW = HD + 1
NB = 72
JG = 20
NEG = -1.0e37
FAR = float(1 << 20)
EPS = 1e-5
SPLIT = 3
PAIRS = 6
AUG = PAIRS * HD + SPLIT
QUADS = [(qt, b) for qt in range(NCH - 1, -1, -1) for b in range(qt + 1)]
NQ = len(QUADS)
TILES = [(i, c) for c in range(NCH - 1, -1, -1) for i in range(4 * c, NT)]
NTL = len(TILES)
CREDIT = 2


def const_layout():
    at, cols = {}, 0
    for name, width in (("ident", P), ("tri", P), ("sel", VW), ("mult", 3 * NT), ("eid", E), ("grid", JG),
                        ("block", NB), ("tok", NT), ("scan", TOPK * E * NT), ("maskT", 4 * P), ("maskS", P)):
        at[name] = (cols, width)
        cols += width
    return at, cols


def const_array():
    at, cols = const_layout()
    c = np.zeros((P, cols), np.float32)

    def put(name, value):
        a, w = at[name]
        c[:, a:a + w] = np.broadcast_to(value, (P, w))

    r = np.arange(P)
    put("ident", np.eye(P))
    put("tri", r[:, None] < r[None, :])
    sel = np.zeros((P, VW))
    for g in range(4):
        sel[32 * g + np.arange(VW), np.arange(VW)] = 1.0
    put("sel", sel)
    first, second = S // 3, 2 * S // 3
    pos = r[:, None] + P * np.arange(NT)[None, :]
    regions = [pos < first, (pos >= first) & (pos < second), pos >= second]
    put("mult", np.concatenate([np.float32(1.0) + np.float32(0.6) * g.astype(np.float32) for g in regions], 1))
    put("eid", np.arange(E) - E)
    put("grid", P * np.arange(JG))
    put("block", np.arange(NB))
    put("tok", pos)
    put("scan", (np.arange(TOPK * E * NT) % NT != 0))
    put("maskT", np.where(r[:, None] > np.arange(-3 * P, P)[None, :], NEG, 0.0))
    put("maskS", np.where(r[None, :] > r[:, None], NEG, 0.0))
    return c


def build(nc, x, w_attn, b_attn, b_qk, w_proj, b_proj, w_router, w1, w2, consts, out):
    at, CW = const_layout()
    from contextlib import ExitStack
    ctx = ExitStack()
    with ctx:
        def sb(name, shape, dt=F32, scope=ctx):
            return scope.enter_context(nc.sbuf_tensor(name, shape, dt))

        def sem(name):
            return ctx.enter_context(nc.semaphore(name))

        def sems(name, n=2):
            return [sem(f"{name}{j}") for j in range(n)]

        x_rows = x.rearrange("a s d -> (a s) d")
        out_rows = out.rearrange("a s d -> (a s) d")
        xn_dram = nc.dram_tensor("xn_scratch", [S, D], F32, kind="Internal").ap()
        qk_dram = nc.dram_tensor("qk_scratch", [2, SPLIT, D, S], BF16, kind="Internal").ap()
        list_dram = nc.dram_tensor("list_scratch", [NB * P, 1], F32, kind="Internal").ap()
        y_dram = nc.dram_tensor("y_scratch", [NB * P, D], F32, kind="Internal").ap()

        cst = sb("cst", [P, CW])

        def con(name):
            a, w = at[name]
            return cst[:, a:a + w]

        ident = con("ident")
        identb = sb("identb", [P, P], BF16)
        maskT = sb("maskT", [P, 4 * P], BF16)
        maskS = sb("maskS", [P, P], BF16)
        ones = sb("ones", [P, P])
        eps = sb("eps", [P, 1])
        wqk = sb("wqk", [P, KD, 2 * D])
        wv = sb("wv", [P, KD, D + E])
        bv = sb("bv", [1, D + E])
        bqk = sb("bqk", [P, 4])
        bqk4 = sb("bqk4", [P, 4])
        wp = sb("wp", [P, KD, D])
        bp = sb("bp", [1, D])
        v_all = sb("v_all", [P, H, NT, VW])
        logits = sb("logits", [P, NT, E])
        gates = sb("gates", [P, TOPK, NT])
        slot_out = sb("slot_out", [P, TOPK, NT], I32)
        slot_in = sb("slot_in", [P, TOPK, NT], I32)
        expert_of = sb("expert_of", [P, NB], I32)

        passed = {name: sem(f"passed_{name}") for name in ("sp", "pool", "dve")}

        def wait_apart(eng, name, semaphore, value):
            eng.wait_ge(semaphore, value)
            eng.sem_inc(passed[name], 1)

        s_const = sem("s_const")
        s_vec0 = sem("s_vec0")
        s_pool0 = sem("s_pool0")

        weights = ctx.enter_context(ExitStack())
        w1_sb = sb("w1_sb", [P, KD, E, F], scope=weights)
        w2_sb = sb("w2_sb", [P, E, KF, D], scope=weights)
        lent = w2_sb[:].rearrange("p e k d -> p (e k d)")
        xT_all = lent[:, E * F // 2 * KD:].rearrange("p (k s) -> p k s", k=KD)
        half = 4 * D
        x_st = [lent[:, j * half:(j + 1) * half].rearrange("p (b d) -> p b d", b=4) for j in (0, 1)]
        xn_st = [lent[:, j * half:(j + 1) * half].rearrange("p (b d) -> p b d", b=4) for j in (2, 3)]
        xT_st = [lent[:, j * half:(j + 1) * half].rearrange("p (k s) -> p k s", k=KD) for j in (4, 5)]
        w1_dram = w1.rearrange("e (k p) f -> e p k f", p=P)
        w2_dram = w2.rearrange("e (k p) d -> e p k d", p=P)

        w1_loaded = sem("w1_loaded")
        w2_loaded = sem("w2_loaded")

        def stage_tokens():
            scope = ExitStack()
            with scope:
                stats = [sb(f"stats{j}", [P, 4, 6], scope=scope) for j in range(2)]
                mv = [sb(f"mv{j}", [P, 4, 2], scope=scope) for j in range(2)]
                std = [sb(f"std{j}", [P, 4], scope=scope) for j in range(2)]
                rstd = [sb(f"rstd{j}", [P, 4], scope=scope) for j in range(2)]
                psT = [scope.enter_context(nc.psum_tensor(f"psT{j}", [P, KD, CH], F32)) for j in range(2)]
                psV = scope.enter_context(nc.psum_tensor("psV", [P, 4, CH], F32))
                x_loaded = sems("x_loaded")
                st_ready, mv_ready, std_ready = sem("st_ready"), sems("mv_ready"), sems("std_ready")
                rstd_ready = sem("rstd_ready")
                xn_ready, xn_stored = sems("xn_ready"), sems("xn_stored")
                xT_in_psum, xT_ready, xT_kept = sems("xT_in_psum"), sems("xT_ready"), sems("xT_kept")
                v_in_psum, v_out_act, v_out_dve = sem("v_in_psum"), sem("v_out_act"), sem("v_out_dve")
                x_blocks = x_rows.rearrange("(c b p) d -> c p b d", p=P, b=4)
                xn_blocks = xn_dram.rearrange("(c b p) d -> c p b d", p=P, b=4)
                block = scope.enter_context(nc.Block())

                @block.sync
                def _(sp):
                    sp.dma_start(cst[:], consts).then_inc(s_const, 16)
                    sp.dma_start(wv[:, :, 0:D], w_attn[:, 2 * D:3 * D].rearrange("(k p) n -> p k n", p=P)).then_inc(s_const, 16)
                    sp.dma_start(wv[:, :, D:D + E], w_router.rearrange("(k p) e -> p k e", p=P)).then_inc(s_const, 16)
                    sp.dma_start(bv[:, 0:D], b_attn[:, 2 * D:3 * D]).then_inc(s_const, 16)
                    with sp.Fori(0, NCH // 2) as i:
                        for j in (0, 1):
                            sp.wait_ge(xn_ready[j], 4 * i)
                            sp.dma_start(x_st[j], x_blocks[bass.ds(2 * i + j, 1)].rearrange("c p b d -> (c p) b d")).then_inc(x_loaded[j], 16)
                            sp.dma_start(w1_sb[:, :, bass.ds(2 * i + j, 1), :].rearrange("p k e f -> p (k e) f"),
                                         w1_dram[bass.ds(2 * i + j, 1)].rearrange("e p k f -> (e p) k f")).then_inc(w1_loaded, 16)
                    sp.dma_start(wqk[:], w_attn[:, 0:2 * D].rearrange("(k p) n -> p k n", p=P)).then_inc(s_const, 16)
                    sp.dma_start(bqk[:], b_qk).then_inc(s_const, 16)
                    sp.dma_start(wp[:], w_proj.rearrange("(k p) n -> p k n", p=P)).then_inc(s_const, 16)
                    sp.dma_start(bp[:], b_proj).then_inc(s_const, 16)

                @block.gpsimd
                def _(pool):
                    pool.memset(ones[:], 1.0).then_inc(s_pool0, 1)
                    pool.memset(eps[:], EPS).then_inc(s_pool0, 1)
                    pool.memset(bv[:, D:D + E], 0.0).then_inc(s_pool0, 1)
                    pool.memset(v_all[:, :, :, HD:VW], 1.0).then_inc(s_pool0, 1)
                    with pool.Fori(0, NCH // 2) as i:
                        for j in (0, 1):
                            pool.wait_ge(xT_ready[j], 2 * i + 2)
                            pool.tensor_copy(xT_all[:, :, bass.ds((2 * i + j) * CH, CH)], xT_st[j]).then_inc(xT_kept[j], 1)

                @block.vector
                def _(dve):
                    dve.wait_ge(s_const, 64)
                    dve.tensor_copy(identb[:], ident).then_inc(s_vec0, 1)
                    dve.tensor_copy(maskT[:], con("maskT")).then_inc(s_vec0, 1)
                    dve.tensor_copy(maskS[:], con("maskS")).then_inc(s_vec0, 1)
                    with dve.Fori(0, NCH // 2) as i:
                        for j in (0, 1):
                            dve.wait_ge(x_loaded[j], 16 * i + 16)
                            for b in range(4):
                                dve.bn_stats(stats[j][:, b, :], x_st[j][:, b, :]).then_inc(st_ready, 1)
                            wait_apart(dve, "dve", st_ready, (2 * i + j) * 4 + 4)
                            for b in range(4):
                                dve.bn_aggr(mv[j][:, b, :], stats[j][:, b, :]).then_inc(mv_ready[j], 1)
                            dve.wait_ge(std_ready[j], i + 1)
                            dve.reciprocal(rstd[j][:], std[j][:]).then_inc(rstd_ready, 1)
                            dve.wait_ge(rstd_ready, 2 * i + j + 1)
                            dve.wait_ge(xT_in_psum[j], i)
                            dve.wait_ge(xn_stored[j], 16 * i)
                            for b in range(4):
                                ins = dve.tensor_scalar(xn_st[j][:, b, :], x_st[j][:, b, :], mv[j][:, b, 0:1],
                                                        rstd[j][:, b:b + 1], ALU.subtract, ALU.mult)
                                ins.then_inc(xn_ready[j], 1)
                            dve.wait_ge(xT_in_psum[j], i + 1)
                            dve.wait_ge(xT_kept[j], i)
                            if j == 0:
                                dve.wait_ge(v_in_psum, 2 * i)
                            else:
                                dve.wait_ge(v_in_psum, 2 * i)
                            dve.tensor_copy(xT_st[j][:, 1, :], psT[j][:, 1, :]).then_inc(xT_ready[j], 1)
                            dve.wait_ge(v_in_psum, 2 * i + j + 1)
                            for b in (2, 3):
                                dve.tensor_copy(v_all[:, :, bass.ds((2 * i + j) * 4 + b, 1), 0:HD].rearrange("p h b d -> p h (b d)"),
                                                psV[:, b, 0:D].rearrange("p (h d) -> p h d", h=H))
                            dve.tensor_copy(logits[:, bass.ds((2 * i + j) * 4 + 2, 2), :], psV[:, 2:4, D:D + E]).then_inc(v_out_dve, 1)

                @block.scalar
                def _(act):
                    act.wait_ge(s_pool0, 4)
                    with act.Fori(0, NCH // 2) as i:
                        for j in (0, 1):
                            act.wait_ge(mv_ready[j], 4 * i + 4)
                            act.wait_ge(rstd_ready, 2 * i)
                            act.activation(std[j][:], mv[j][:, :, 1], ACT.Sqrt, bias=eps[:, 0:1], scale=1.0).then_inc(std_ready[j], 1)
                            act.wait_ge(xn_ready[j], 4 * i + 4)
                            act.dma_start(xn_blocks[bass.ds(2 * i + j, 1)].rearrange("c p b d -> (c p) b d"), xn_st[j]).then_inc(xn_stored[j], 16)
                            act.wait_ge(xT_in_psum[j], i + 1)
                            act.wait_ge(xT_kept[j], i)
                            act.wait_ge(v_in_psum, 2 * i)
                            act.copy(xT_st[j][:, 0, :], psT[j][:, 0, :]).then_inc(xT_ready[j], 1)
                            act.wait_ge(v_in_psum, 2 * i + j + 1)
                            for b in (0, 1):
                                act.copy(v_all[:, :, bass.ds((2 * i + j) * 4 + b, 1), 0:HD].rearrange("p h b d -> p h (b d)"),
                                         psV[:, b, 0:D].rearrange("p (h d) -> p h d", h=H))
                            act.copy(logits[:, bass.ds((2 * i + j) * 4, 2), :], psV[:, 0:2, D:D + E]).then_inc(v_out_act, 1)
                    act.wait_ge(xn_stored[0], 16 * (NCH // 2))
                    act.wait_ge(xn_stored[1], 16 * (NCH // 2))

                @block.tensor
                def _(pe):
                    pe.wait_ge(s_const, 64)
                    pe.wait_ge(s_pool0, 4)
                    with pe.Fori(0, NCH // 2) as i:
                        for j in (0, 1):
                            pe.wait_ge(xn_ready[j], 4 * i + 4)
                            pe.wait_ge(xT_ready[j], 2 * i)
                            for k in range(KD):
                                for b in range(4):
                                    ins = pe.transpose(psT[j][:, k, b * P:(b + 1) * P], xn_st[j][:, b, k * P:(k + 1) * P], ident)
                            ins.then_inc(xT_in_psum[j], 1)
                            pe.wait_ge(xT_ready[j], 2 * i + 2)
                            pe.wait_ge(v_out_act, 2 * i + j)
                            pe.wait_ge(v_out_dve, 2 * i + j)
                            for b in range(4):
                                pe.matmul(psV[:, b, 0:D + E], ones[0:1, :], bv[:], start=True, stop=False)
                                for k in range(KD):
                                    ins = pe.matmul(psV[:, b, 0:D + E], xT_st[j][:, k, b * P:(b + 1) * P], wv[:, k, :],
                                                    start=False, stop=(k == KD - 1))
                            ins.then_inc(v_in_psum, 1)

        def stage_queries():
            scope = ExitStack()
            with scope:
                t_st = [sb(f"t_st{q}", [P, CH], scope=scope) for q in range(2)]
                r_both = sb("r_both", [P, 2 * CH], scope=scope)
                r_st = [r_both[:, q * CH:(q + 1) * CH] for q in range(2)]
                s_st = [sb(f"s_st{q}", [P, SPLIT, CH], BF16, scope=scope) for q in range(2)]
                big = TOPK * NT * E
                onehot = sb("onehot", [P, TOPK, NT, E], scope=scope)
                tmp = sb("tmp", [P, TOPK, NT, E], scope=scope)
                cnt = sb("cnt", [P, TOPK, E, NT], scope=scope)
                inc = sb("inc", [P, TOPK, E, NT], scope=scope)
                m1 = sb("m1", [P, NT], scope=scope)
                m2 = sb("m2", [P, NT], scope=scope)
                fst = sb("fst", [P, NT], scope=scope)
                e2 = sb("e2", [P, NT], scope=scope)
                pos = sb("pos", [P, TOPK, NT], scope=scope)
                keep = sb("keep", [P, TOPK, NT], scope=scope)
                tot = sb("tot", [P, TOPK, E], scope=scope)
                nsum = sb("nsum", [P, E], scope=scope)
                nblk = sb("nblk", [P, E], scope=scope)
                endb = sb("endb", [P, E], scope=scope)
                base = sb("base", [P, TOPK, E], scope=scope)
                blk = r_both[:, 0:NB * E].rearrange("p (b e) -> p b e", e=E)
                eidf = sb("eidf", [P, NB], scope=scope)
                zero = sb("zero", [NB, P], scope=scope)
                sidx = [sb(f"sidx{k}", [P, 1], I32, scope=scope) for k in range(TOPK)]
                stok = [sb(f"stok{k}", [P, 1], scope=scope) for k in range(TOPK)]
                psQ = [scope.enter_context(nc.psum_tensor(f"psQ{q}", [P, CH], F32)) for q in range(2)]
                psR = [scope.enter_context(nc.psum_tensor(f"psR{q}", [P, TOPK, NT, E], F32)) for q in range(2)]
                q_in_psum, t_ready, s1_ready = sems("q_in_psum"), sems("t_ready"), sems("s1_ready")
                r_ready, s2_ready, s3_ready, q_stored = sems("r_ready"), sems("s2_ready"), sems("s3_ready"), sems("q_stored")
                counted, gap_ready, e2_ready = sem("counted"), sem("gap_ready"), sem("e2_ready")
                ONEHOT_LINKS = 11
                slots_ready, zero_ready, listed = sem("slots_ready"), sem("zero_ready"), sems("listed")
                idx_ready, route = sem("idx_ready"), sem("route")
                list_zeroed = sem("list_zeroed")
                units = [(fc, fc % 2, fc // 2) for fc in range(4)]
                block = scope.enter_context(nc.Block())

                @block.sync
                def _(sp):
                    for e in range(E // 2):
                        sp.dma_start(w2_sb[:, e], w2_dram[e]).then_inc(w2_loaded, 16)
                    sp.wait_ge(zero_ready, 1)
                    sp.dma_start(list_dram.rearrange("(b p) o -> b (p o)", p=P), zero[:]).then_inc(list_zeroed, 16)
                    with sp.Fori(0, NCH) as i:
                        for fc, q, r in units:
                            sp.wait_ge(s3_ready[q], 2 * i + r + 1)
                            dst = qk_dram[fc // 2, :, (fc % 2) * P:(fc % 2 + 1) * P, bass.ds(i * CH, CH)]
                            sp.dma_start(dst.rearrange("c p s -> p c s"), s_st[q][:]).then_inc(q_stored[q], 16)
                    for q in range(2):
                        sp.wait_ge(q_stored[q], 16 * 2 * NCH)

                @block.gpsimd
                def _(pool):
                    pool.memset(zero[:], 0.0).then_inc(zero_ready, 1)
                    pool.wait_ge(list_zeroed, 16)
                    pool.wait_ge(slots_ready, 2)
                    with pool.Fori(0, NT) as i:
                        for k in range(TOPK):
                            pool.wait_ge(listed[k], 16 * i)
                            pool.tensor_copy(sidx[k][:], slot_out[:, k, bass.ds(i, 1)]).then_inc(idx_ready, 1)
                            pool.tensor_copy(stok[k][:], con("tok")[:, bass.ds(i, 1)]).then_inc(idx_ready, 1)
                            wait_apart(pool, "pool", idx_ready, 4 * i + 2 * k + 2)
                            pool.indirect_dma_start(out=list_dram, out_offset=bass.IndirectOffsetOnAxis(ap=sidx[k][:, 0:1], axis=0),
                                                    in_=stok[k][:], in_offset=None, bounds_check=NB * P - 1,
                                                    oob_is_err=False).then_inc(listed[k], 16)
                    for k in range(TOPK):
                        pool.wait_ge(listed[k], 16 * NT)

                @block.scalar
                def _(act):
                    act.wait_ge(s_const, 128)
                    act.mul(bqk4[:, 0:2], bqk[:, 0:2], 0.25)
                    act.copy(bqk4[:, 2:4], bqk[:, 2:4]).then_inc(s_vec0, 1)
                    act.wait_ge(s_vec0, 4)
                    act.wait_ge(gap_ready, 1)
                    act.activation(e2[:], e2[:], ACT.Exp).then_inc(e2_ready, 1)
                    with act.Fori(0, NCH) as i:
                        for fc, q, r in units:
                            act.wait_ge(q_in_psum[q], 2 * i + r + 1)
                            act.wait_ge(r_ready[q], 2 * i + r)
                            act.activation(t_st[q][:], psQ[q][:], ACT.Identity, bias=bqk4[:, fc:fc + 1],
                                           scale=0.25 if fc < 2 else 1.0).then_inc(t_ready[q], 1)
                            act.wait_ge(t_ready[q], 2 * i + r + 1)
                            act.wait_ge(q_stored[q], 32 * i + 16 * r)
                            act.copy(s_st[q][:, 0, :], t_st[q][:]).then_inc(s1_ready[q], 1)

                @block.vector
                def _(dve):
                    n = [0]

                    def link(ins):
                        n[0] += 1
                        ins.then_inc(route, 1)
                        dve.wait_ge(route, n[0])

                    def wide(a, shape):
                        return a.to_broadcast(shape)

                    eid = con("eid")
                    SH = [P, NT, E]
                    lg = logits[:]
                    for k, m in ((0, m1), (1, m2)):
                        link(dve.tensor_reduce(m[:], lg, AX, ALU.max))
                        link(dve.tensor_tensor(tmp[:, 0], lg, wide(m[:].unsqueeze(2), SH), ALU.is_equal))
                        link(dve.tensor_tensor(tmp[:, 0], tmp[:, 0], wide(eid.unsqueeze(1), SH), ALU.mult))
                        link(dve.tensor_reduce(fst[:], tmp[:, 0], AX, ALU.min))
                        link(dve.tensor_tensor(onehot[:, k], wide(eid.unsqueeze(1), SH), wide(fst[:].unsqueeze(2), SH), ALU.is_equal))
                        if k == 0:
                            link(dve.scalar_tensor_tensor(out=tmp[:, 1], in0=onehot[:, 0], scalar=-3.0e38, in1=lg,
                                                          op0=ALU.mult, op1=ALU.add))
                            lg = tmp[:, 1]
                    dve.tensor_tensor(e2[:], m2[:], m1[:], ALU.subtract).then_inc(gap_ready, 1)
                    assert n[0] == ONEHOT_LINKS
                    dve.wait_ge(e2_ready, 1)
                    link(dve.tensor_scalar(m1[:], e2[:], 1.0, None, ALU.add))
                    link(dve.reciprocal(gates[:, 0], m1[:]))
                    link(dve.tensor_tensor(gates[:, 1], e2[:], gates[:, 0], ALU.mult))
                    dve.wait_ge(counted, 2)
                    link(dve.tensor_copy(cnt[:].rearrange("p k e b -> p k b e"), psR[1][:]))
                    f = "p k e b -> p (k e b)"
                    link(dve.tensor_tensor_scan(inc[:].rearrange(f), con("scan"), cnt[:].rearrange(f), 0.0, ALU.mult, ALU.add))
                    link(dve.tensor_scalar(tot[:], inc[:, :, :, NT - 1], float(CAP), None, ALU.min))
                    link(dve.tensor_tensor(inc[:], inc[:], cnt[:], ALU.subtract))
                    for k in range(TOPK):
                        link(dve.tensor_tensor(tmp[:, k], inc[:, k].rearrange("p e b -> p b e"), psR[0][:, k], ALU.add))
                        link(dve.tensor_tensor(tmp[:, k], tmp[:, k], onehot[:, k], ALU.mult))
                        link(dve.tensor_reduce(pos[:, k], tmp[:, k], AX, ALU.add))
                    link(dve.tensor_tensor(nsum[:], tot[:, 0], tot[:, 1], ALU.add))
                    link(dve.tensor_tensor(tmp[:].rearrange("p k b e -> p (k b e)")[:, 0:E * JG].rearrange("p (e j) -> p e j", e=E),
                                           wide(nsum[:].unsqueeze(2), [P, E, JG]), wide(con("grid").unsqueeze(1), [P, E, JG]), ALU.is_gt))
                    link(dve.tensor_reduce(nblk[:], tmp[:].rearrange("p k b e -> p (k b e)")[:, 0:E * JG].rearrange("p (e j) -> p e j", e=E),
                                           AX, ALU.add))
                    link(dve.tensor_tensor_scan(endb[:], ones[:, 0:E], nblk[:], 0.0, ALU.mult, ALU.add))
                    link(dve.tensor_tensor(base[:, 0], endb[:], nblk[:], ALU.subtract))
                    link(dve.tensor_scalar(base[:, 0], base[:, 0], float(P), None, ALU.mult))
                    link(dve.tensor_tensor(base[:, 1], base[:, 0], tot[:, 0], ALU.add))
                    link(dve.tensor_scalar(keep[:], pos[:], float(CAP), None, ALU.is_lt))
                    for k in range(TOPK):
                        link(dve.tensor_tensor(tmp[:, k], onehot[:, k], wide(base[:, k].unsqueeze(1), SH), ALU.mult))
                        link(dve.tensor_reduce(m1[:], tmp[:, k], AX, ALU.add))
                        link(dve.tensor_tensor(pos[:, k], pos[:, k], m1[:], ALU.add))
                    link(dve.tensor_tensor(gates[:], gates[:], keep[:], ALU.mult))
                    link(dve.tensor_tensor(pos[:], pos[:], keep[:], ALU.mult))
                    dve.tensor_copy(slot_in[:], pos[:]).then_inc(slots_ready, 1)
                    link(dve.tensor_scalar(keep[:], keep[:], -FAR, FAR, ALU.mult, ALU.add))
                    link(dve.tensor_tensor(pos[:], pos[:], keep[:], ALU.add))
                    dve.tensor_copy(slot_out[:], pos[:]).then_inc(slots_ready, 1)
                    link(dve.tensor_tensor(blk, wide(endb[:].unsqueeze(1), [P, NB, E]), wide(con("block").unsqueeze(2), [P, NB, E]), ALU.is_le))
                    link(dve.tensor_reduce(eidf[:], blk, AX, ALU.add))
                    link(dve.tensor_scalar(eidf[:], eidf[:], float(E - 1), None, ALU.min))
                    link(dve.tensor_copy(expert_of[:], eidf[:]))
                    dve.wait_ge(s_pool0, 4)
                    for h in range(3):
                        dve.tensor_tensor(v_all[:, h], v_all[:, h],
                                          wide(con("mult")[:, h * NT:(h + 1) * NT].unsqueeze(2), [P, NT, VW]), ALU.mult)
                    with dve.Fori(0, NCH) as i:
                        for fc, q, r in units:
                            dve.wait_ge(s1_ready[q], 2 * i + r + 1)
                            dve.tensor_tensor(r_st[q], t_st[q][:], s_st[q][:, 0, :], ALU.subtract).then_inc(r_ready[q], 1)
                            dve.wait_ge(r_ready[q], 2 * i + r + 1)
                            dve.tensor_copy(s_st[q][:, 1, :], r_st[q]).then_inc(s2_ready[q], 1)
                            dve.wait_ge(s2_ready[q], 2 * i + r + 1)
                            dve.tensor_tensor(s_st[q][:, 2, :], r_st[q], s_st[q][:, 1, :], ALU.subtract).then_inc(s3_ready[q], 1)

                @block.tensor
                def _(pe):
                    pe.wait_ge(s_const, 128)

                    def count():
                        pe.wait_ge(route, ONEHOT_LINKS)
                        rows = onehot[:].rearrange("p k b e -> p (k b e)")
                        pe.matmul(psR[0][:].rearrange("p k b e -> p (k b e)"), con("tri"), rows, start=True, stop=True).then_inc(counted, 1)
                        pe.matmul(psR[1][:].rearrange("p k b e -> p (k b e)"), ones[:], rows, start=True, stop=True).then_inc(counted, 1)

                    count()
                    with pe.Fori(0, NCH) as i:
                        for fc, q, r in units:
                            pe.wait_ge(t_ready[q], 2 * i + r)
                            for k in range(KD):
                                ins = pe.matmul(psQ[q][:], wqk[:, k, fc * P:(fc + 1) * P], xT_all[:, k, bass.ds(i * CH, CH)],
                                                start=(k == 0), stop=(k == KD - 1))
                            ins.then_inc(q_in_psum[q], 1)

        def stage_experts():
            scope = ExitStack()
            with scope:
                listed_rows = sb("listed_rows", [NB, P], scope=scope)
                tokens = sb("tokens", [P, NB], I32, scope=scope)
                gidx = [sb(f"gidx{j}", [P, 1], I32, scope=scope) for j in range(2)]
                xg = [sb(f"xg{j}", [P, D], scope=scope) for j in range(2)]
                xgT = [sb(f"xgT{j}", [P, KD, P], scope=scope) for j in range(2)]
                h_sb = sb("h_sb", [P, F], scope=scope)
                hT = sb("hT", [P, KF, P], scope=scope)
                y_sb = [sb(f"y_sb{j}", [P, D], scope=scope) for j in range(2)]
                psX = scope.enter_context(nc.psum_tensor("psX", [P, CH], F32))
                psH = scope.enter_context(nc.psum_tensor("psH", [P, F], F32))
                psHT = scope.enter_context(nc.psum_tensor("psHT", [P, KF, P], F32))
                psY = [scope.enter_context(nc.psum_tensor(f"psY{j}", [P, CH], F32)) for j in range(2)]
                list_loaded, list_turned, tokens_ready = sem("list_loaded"), sem("list_turned"), sem("tokens_ready")
                gidx_ready, gathered = sems("gidx_ready"), sems("gathered")
                x_turned, xgT_ready = sem("x_turned"), sem("xgT_ready")
                h_in_psum, h_ready, h_turned, hT_ready = sem("h_in_psum"), sem("h_ready"), sem("h_turned"), sem("hT_ready")
                y_in_psum, y_ready, y_stored = sem("y_in_psum"), sem("y_ready"), sems("y_stored")
                block = scope.enter_context(nc.Block())
                NI = NB // 2

                @block.sync
                def _(sp):
                    sp.dma_start(listed_rows[:], list_dram.rearrange("(b p) o -> b (p o)", p=P)).then_inc(list_loaded, 16)
                    for e in range(E // 2, E):
                        sp.dma_start(w2_sb[:, e], w2_dram[e]).then_inc(w2_loaded, 16)
                    with sp.Fori(0, NI) as i:
                        for j in (0, 1):
                            sp.wait_ge(y_ready, 2 * i + j + 1)
                            sp.dma_start(y_dram[bass.ds((2 * i + j) * P, P), :], y_sb[j][:]).then_inc(y_stored[j], 16)
                    for j in (0, 1):
                        sp.wait_ge(y_stored[j], 16 * NI)

                @block.gpsimd
                def _(pool):
                    pool.wait_ge(tokens_ready, 1)
                    with pool.Fori(0, NI) as i:
                        for j in (0, 1):
                            if j == 0:
                                pool.wait_ge(x_turned, 2 * i)
                            else:
                                pool.wait_ge(x_turned, 2 * i)
                            pool.wait_ge(gathered[j], 16 * i)
                            pool.tensor_copy(gidx[j][:], tokens[:, bass.ds(2 * i + j, 1)]).then_inc(gidx_ready[j], 1)
                            wait_apart(pool, "pool", gidx_ready[j], i + 1)
                            pool.indirect_dma_start(out=xg[j][:], out_offset=None, in_=xn_dram,
                                                    in_offset=bass.IndirectOffsetOnAxis(ap=gidx[j][:, 0:1], axis=0),
                                                    bounds_check=S - 1, oob_is_err=False).then_inc(gathered[j], 16)

                @block.vector
                def _(dve):
                    dve.wait_ge(list_turned, 1)
                    dve.tensor_copy(tokens[:], psX[:, 0:NB]).then_inc(tokens_ready, 1)

                    def x_copy(n, j):
                        dve.wait_ge(x_turned, n + 1)
                        dve.tensor_copy(xgT[j][:], psX[:, 0:D].rearrange("p (k t) -> p k t", k=KD)).then_inc(xgT_ready, 1)

                    x_copy(0, 0)
                    x_copy(1, 1)
                    with dve.Fori(0, NI - 1) as i:
                        for j in (0, 1):
                            dve.wait_ge(h_turned, 2 * i + j + 1)
                            dve.tensor_copy(hT[:], psHT[:]).then_inc(hT_ready, 1)
                            dve.wait_ge(h_in_psum, 2 * i + j + 1)
                            x_copy(2 * i + j + 2, j)
                    for n in (NB - 2, NB - 1):
                        dve.wait_ge(h_turned, n + 1)
                        dve.tensor_copy(hT[:], psHT[:]).then_inc(hT_ready, 1)

                @block.scalar
                def _(act):
                    def gelu(n):
                        act.wait_ge(h_in_psum, n + 1)
                        act.wait_ge(h_turned, n)
                        act.activation(h_sb[:], psH[:], ACT.Gelu).then_inc(h_ready, 1)

                    def y_copy(n, i, j):
                        act.wait_ge(y_in_psum, n + 1)
                        act.wait_ge(y_stored[j], 16 * i)
                        act.copy(y_sb[j][:], psY[j][:, 0:D]).then_inc(y_ready, 1)

                    gelu(0)
                    with act.Fori(0, NI - 1) as i:
                        for j in (0, 1):
                            gelu(2 * i + j + 1)
                            y_copy(2 * i + j, i, j)
                    gelu(NB - 1)
                    y_copy(NB - 2, NI - 1, 0)
                    y_copy(NB - 1, NI - 1, 1)

                @block.tensor
                def _(pe):
                    pe.wait_ge(list_loaded, 16)
                    pe.transpose(psX[:, 0:NB], listed_rows[:], ident[0:NB, 0:NB]).then_inc(list_turned, 1)
                    pe.wait_ge(tokens_ready, 1)

                    def turn_x(n, i, j):
                        pe.wait_ge(gathered[j], 16 * i + 16)
                        pe.wait_ge(xgT_ready, n)
                        for k in range(KD):
                            ins = pe.transpose(psX[:, k * P:(k + 1) * P], xg[j][:, k * P:(k + 1) * P], ident)
                        ins.then_inc(x_turned, 1)

                    def first(n, j):
                        expert = pe.value_load(expert_of[0:1, bass.ds(n, 1)], min_val=0, max_val=E - 1)
                        pe.wait_ge(xgT_ready, n + 1)
                        pe.wait_ge(h_ready, n)
                        for k in range(KD):
                            for c in range(F // CH):
                                ins = pe.matmul(psH[:, c * CH:(c + 1) * CH], xgT[j][:, k, :],
                                                w1_sb[:, k, bass.ds(expert, 1), c * CH:(c + 1) * CH].rearrange("p e f -> p (e f)"),
                                                start=(k == 0), stop=(k == KD - 1))
                        ins.then_inc(h_in_psum, 1)

                    def turn_h(n):
                        pe.wait_ge(h_ready, n + 1)
                        pe.wait_ge(hT_ready, n)
                        for k in range(KF):
                            ins = pe.transpose(psHT[:, k, :], h_sb[:, k * P:(k + 1) * P], ident)
                        ins.then_inc(h_turned, 1)

                    def second(n, i, j):
                        expert = pe.value_load(expert_of[0:1, bass.ds(n, 1)], min_val=0, max_val=E - 1)
                        pe.wait_ge(hT_ready, n + 1)
                        if j == 0:
                            pe.wait_ge(y_ready, 2 * i)
                        else:
                            pe.wait_ge(y_ready, 2 * i)
                        for k in range(KF):
                            ins = pe.matmul(psY[j][:, 0:D], hT[:, k, :],
                                            w2_sb[:, bass.ds(expert, 1), k, :].rearrange("p e d -> p (e d)"),
                                            start=(k == 0), stop=(k == KF - 1))
                        ins.then_inc(y_in_psum, 1)

                    turn_x(0, 0, 0)
                    pe.wait_ge(w1_loaded, 16 * E)
                    first(0, 0)
                    turn_x(1, 0, 1)
                    pe.wait_ge(w2_loaded, 16 * E)
                    with pe.Fori(0, NI - 1) as i:
                        for j in (0, 1):
                            turn_h(2 * i + j)
                            first(2 * i + j + 1, 1 - j)
                            second(2 * i + j, i, j)
                            turn_x(2 * i + j + 2, i + 1, j)
                    turn_h(NB - 2)
                    first(NB - 1, 1)
                    second(NB - 2, NI - 1, 0)
                    turn_h(NB - 1)
                    second(NB - 1, NI - 1, 1)

        def stage_attend(attn):
            scope = ExitStack()
            with scope:
                qa = [sb(f"qa{j}", [AUG, S], BF16, scope=scope) for j in range(2)]
                ka = [sb(f"ka{j}", [AUG, S], BF16, scope=scope) for j in range(2)]
                vh = [sb(f"vh{j}", [P, NT, 32], scope=scope) for j in range(2)]
                probs = [sb(f"probs{j}", [P, 4, CH], scope=scope) for j in range(2)]
                oT = [sb(f"oT{j}", [P, CH], scope=scope) for j in range(2)]
                rden = sb("rden", [P, 4, 1], scope=scope)
                mxp = sb("mxp", [P, NT, NCH], scope=scope)
                nm = sb("nm", [P, NT], scope=scope)
                nr = sb("nr", [P, NT], scope=scope)
                nm3 = sb("nm3", [P, SPLIT, NT], BF16, scope=scope)
                mT = sb("mT", [SPLIT * NT, P], BF16, scope=scope)
                psS = scope.enter_context(nc.psum_tensor("psS", [P, 4, CH], F32))
                psM = [scope.enter_context(nc.psum_tensor(f"psM{j}", [P, CH], F32)) for j in range(2)]
                psO = scope.enter_context(nc.psum_tensor("psO", [P, CH], F32))
                psN = scope.enter_context(nc.psum_tensor("psN", [P, CH], F32))
                psMT = psN[:].bitcast(BF16)[0:SPLIT * NT, CH:CH + P]
                aug_ones, pads, loaded = sem("aug_ones"), sem("pads"), sems("loaded")
                v_ready = sem("v_ready")
                s_ready, exp_done, pv_done = sem("s_ready"), sem("exp_done"), sem("pv_done")
                o_copied, o_turned, normed, recip = sem("o_copied"), sem("o_turned"), sem("normed"), sem("recip")
                m_ready, m_done, m_chain = sem("m_ready"), sem("m_done"), sem("m_chain")
                negm_ready, negm_turned, negm_copied, negm_loaded = (
                    sem("negm_ready"), sem("negm_turned"), sem("negm_copied"), sem("negm_loaded"))
                M_LINKS = 6
                NI = H // 2 - 1
                LOADS = 6 * 4 * 16
                block = scope.enter_context(nc.Block())

                def heads(eng, step):
                    with eng.Fori(0, NI) as i:
                        step(2 * i, 0, 2 * i + 1, i)
                        step(2 * i + 1, 1, 2 * i + 2, i)
                    step(H - 2, 0, H - 1, NI)
                    step(H - 1, 1, None, NI)

                def tiles_of(u):
                    n = NQ - 3
                    return range(NTL * min(u, n) // n, NTL * min(u + 1, n) // n)

                def ends_tile(u):
                    return u == NQ - 1 or QUADS[u + 1][0] != QUADS[u][0]

                def shape(u):
                    qt, b = QUADS[u]
                    if b < qt or qt == 0:
                        return [(g, 0, CH) for g in range(4)], [2 * CH, 2 * CH]
                    return [(0, 0, CH), (1, 0, 3 * P), (2, 0, 2 * P), (2, 2 * P, P)], [7 * P, 3 * P]

                @block.sync
                def _(sp):
                    def load(g, j, step):
                        cols = slice((3 - step) * 2 * CH, (4 - step) * 2 * CH)
                        f = bass.ds(g * HD, HD)
                        r = 0
                        for which in range(SPLIT):
                            n = SPLIT - which
                            sp.dma_start(qa[j][r:r + n * HD, cols], qk_dram[0, 0:n, f, cols]).then_inc(loaded[j], 16)
                            sp.dma_start(ka[j][r:r + n * HD, cols],
                                         qk_dram[1, which:which + 1, f, cols].to_broadcast([n, HD, 2 * CH])).then_inc(loaded[j], 16)
                            r += n * HD

                    def negm(g, j):
                        sp.wait_ge(negm_copied, g + 1)
                        for c in range(SPLIT):
                            sp.dma_start(qa[j][PAIRS * HD + c:PAIRS * HD + c + 1, :].rearrange("c (b q) -> c b q", q=P),
                                         mT[c * NT:(c + 1) * NT, :]).then_inc(negm_loaded, 16)

                    for g in (0, 1):
                        for step in range(4):
                            load(g, g, step)
                    negm(0, 0)

                    def step(h, j, g, i):
                        for part in range(4):
                            last = max(u for u in range(NQ) if QUADS[u][0] == 6 - 2 * part)
                            if g is not None and not isinstance(g, int):
                                wait_apart(sp, "sp", pv_done, NQ * h + last + 1 + CREDIT)
                                load(h + 2, j, part)
                            if part == 2 and g is not None:
                                negm(g, 1 - j)

                    heads(sp, step)

                @block.gpsimd
                def _(pool):
                    for j in (0, 1):
                        pool.memset(ka[j][PAIRS * HD:AUG, :], 1.0).then_inc(aug_ones, 1)
                    pool.wait_ge(aug_ones, 2)
                    for j in (0, 1):
                        pool.memset(vh[j][:, :, VW:32], 0.0).then_inc(pads, 1)
                    pool.wait_ge(pads, 2)
                    for g in (0, 1):
                        pool.tensor_copy(vh[g][:, :, 0:VW], v_all[:, g]).then_inc(v_ready, 1)

                    def step(h, j, g, i):
                        if g is not None and not isinstance(g, int):
                            pool.wait_ge(pv_done, NQ * h + NQ + CREDIT)
                            pool.tensor_copy(vh[j][:, :, 0:VW], v_all[:, bass.ds(h + 2, 1)].rearrange("p h b d -> p (h b) d")).then_inc(v_ready, 1)

                    heads(pool, step)

                @block.vector
                def _(dve):
                    dve.memset(mxp[:], -3.0e38).then_inc(m_chain, 1)
                    dve.wait_ge(m_chain, 1)
                    dve.sem_inc(m_done, CREDIT)

                    def tile(g, t):
                        i, c = TILES[t]
                        w = min(CH, (i + 1) * P - c * CH)
                        dve.wait_ge(m_ready, NTL * g + t + 1)
                        dve.tensor_reduce(mxp[:, i, c:c + 1], psM[t % 2][:, 0:w], AX, ALU.max).then_inc(m_done, 1)

                    def finish(g):
                        n = [0]

                        def link(ins):
                            n[0] += 1
                            ins.then_inc(m_chain, 1)
                            dve.wait_ge(m_chain, M_LINKS * g + n[0] + 1)

                        dve.wait_ge(m_done, NTL * g + NTL + CREDIT)
                        link(dve.tensor_reduce(nm[:], mxp[:], AX, ALU.max))
                        link(dve.tensor_scalar(nm[:], nm[:], -1.0, None, ALU.mult))
                        dve.wait_ge(negm_turned, g)
                        link(dve.tensor_copy(nm3[:, 0, :], nm[:]))
                        link(dve.tensor_tensor(nr[:], nm[:], nm3[:, 0, :], ALU.subtract))
                        link(dve.tensor_copy(nm3[:, 1, :], nr[:]))
                        link(dve.tensor_tensor(nm3[:, 2, :], nr[:], nm3[:, 1, :], ALU.subtract))
                        assert n[0] == M_LINKS
                        dve.wait_ge(negm_turned, g + 1)
                        dve.wait_ge(negm_loaded, 16 * SPLIT * g)
                        dve.tensor_copy(mT[:], psMT).then_inc(negm_copied, 1)

                    def normalize(h, qt, q):
                        dve.wait_ge(o_turned, q + 1 + CREDIT)
                        o = psN[:, 0:P].rearrange("p (b d) -> p b d", b=4)
                        dve.reciprocal(rden[:], o[:, :, HD:VW]).then_inc(recip, 1)
                        dve.wait_ge(recip, q + 1)
                        dve.tensor_tensor(attn[:, 4 * qt:4 * qt + 4, bass.ds(h * HD, HD)], o[:, :, 0:HD],
                                          rden[:].to_broadcast([P, 4, HD]), ALU.mult).then_inc(normed, 1)

                    for t in range(NTL):
                        tile(0, t)
                    finish(0)

                    def step(h, j, g, i):
                        for u in range(NQ):
                            if g is not None:
                                for t in tiles_of(u):
                                    tile(g, t)
                                if u == NQ - 4:
                                    finish(g)
                            if u >= 2 and ends_tile(u - 2):
                                qt = QUADS[u - 2][0]
                                normalize(h, qt, NCH * h + NCH - 1 - qt)
                        for u in (NQ - 2, NQ - 1):
                            if ends_tile(u):
                                qt = QUADS[u][0]
                                normalize(h, qt, NCH * h + NCH - 1 - qt)

                    heads(dve, step)

                @block.scalar
                def _(act):
                    act.sem_inc(exp_done, CREDIT)

                    def exps(h, u):
                        widths = shape(u)[1]
                        for half in (0, 1):
                            act.wait_ge(s_ready, 2 * (NQ * h + u) + half + 1)
                            if half == 0:
                                act.wait_ge(pv_done, NQ * h + u + 1)
                            w = widths[half]
                            src = psS[:, 2 * half:2 * half + 2, :].rearrange("p a s -> p (a s)")[:, 0:w]
                            dst = probs[u % 2][:, 2 * half:2 * half + 2, :].rearrange("p a s -> p (a s)")[:, 0:w]
                            act.activation(dst, src, ACT.Exp).then_inc(exp_done, 1)

                    def o_copy(h, u):
                        q = NCH * h + NCH - 1 - QUADS[u][0]
                        act.wait_ge(pv_done, NQ * h + u + 1 + CREDIT)
                        act.wait_ge(o_turned, q + 1)
                        act.copy(oT[(NCH - 1 - QUADS[u][0]) % 2][:], psO[:]).then_inc(o_copied, 1)

                    def step(h, j, g, i):
                        for u in range(NQ):
                            exps(h, u)
                            if u >= 1 and ends_tile(u - 1):
                                o_copy(h, u - 1)
                        o_copy(h, NQ - 1)

                    heads(act, step)

                @block.tensor
                def _(pe):
                    pe.sem_inc(pv_done, CREDIT)
                    pe.sem_inc(o_turned, CREDIT)
                    pe.wait_ge(aug_ones, 2)
                    pe.wait_ge(pads, 2)

                    def tile(g, jg, t):
                        i, c = TILES[t]
                        w = min(CH, (i + 1) * P - c * CH)
                        diagonal = c == i // 4
                        pe.wait_ge(m_done, NTL * g + t + 1)
                        ins = pe.matmul(psM[t % 2][:, 0:w], qa[jg][0:PAIRS * HD, i * P:(i + 1) * P], ka[jg][0:PAIRS * HD, c * CH:c * CH + w],
                                        start=True, stop=not diagonal)
                        if diagonal:
                            ins = pe.matmul(psM[t % 2][:, w - P:w], identb[:], maskS[:], start=False, stop=True)
                        ins.then_inc(m_ready, 1)

                    def scores(h, j, u, half):
                        qt, b = QUADS[u]
                        places = shape(u)[0]
                        pe.wait_ge(exp_done, 2 * (NQ * h + u) + half + 1)
                        for g in (2 * half, 2 * half + 1):
                            kb = 4 * b + g
                            bank, col, w = places[g]
                            ins = pe.matmul(psS[:, bank, col:col + w], ka[j][:, kb * P:(kb + 1) * P],
                                            qa[j][:, (qt + 1) * CH - w:(qt + 1) * CH], start=True, stop=b < qt)
                            if b == qt:
                                m = P if w < CH or g == 0 else (g + 1) * P
                                ins = pe.matmul(psS[:, bank, col:col + m], identb[:], maskT[:, 4 * P - m:4 * P], start=False, stop=True)
                        ins.then_inc(s_ready, 1)

                    def products(h, j, u):
                        qt, b = QUADS[u]
                        places = shape(u)[0]
                        pe.wait_ge(exp_done, 2 * (NQ * h + u) + 2 + CREDIT)
                        if b == 0:
                            pe.wait_ge(o_copied, NCH * h + NCH - 1 - qt)
                        for g in range(4):
                            bank, col, w = places[g]
                            ins = pe.matmul(psO[32 * g:32 * g + 32, CH - w:CH], vh[j][:, 4 * b + g, :],
                                            probs[u % 2][:, bank, col:col + w], start=(b == 0), stop=(b == qt),
                                            tile_position=(0, 32 * g))
                        ins.then_inc(pv_done, 1)

                    def turn(h, u):
                        qt = QUADS[u][0]
                        q = NCH * h + NCH - 1 - qt
                        pe.wait_ge(o_copied, q + 1)
                        pe.wait_ge(normed, q)
                        for b in range(4):
                            ins = pe.matmul(psN[:, 32 * b:32 * b + VW], oT[(NCH - 1 - qt) % 2][:, b * P:(b + 1) * P], con("sel"),
                                            start=True, stop=True)
                        ins.then_inc(o_turned, 1)

                    def turn_negm(g, n):
                        pe.wait_ge(m_chain, M_LINKS * g + M_LINKS + 1)
                        pe.wait_ge(normed, n)
                        pe.transpose(psMT, nm3[:].rearrange("p c b -> p (c b)"), identb[:]).then_inc(negm_turned, 1)

                    pe.wait_ge(loaded[0], LOADS)
                    pe.wait_ge(loaded[1], LOADS)
                    for t in range(NTL):
                        tile(0, 0, t)
                    turn_negm(0, 0)

                    def step(h, j, g, i):
                        pe.wait_ge(negm_loaded, 16 * SPLIT * (h + 1))
                        pe.wait_ge(v_ready, h + 1)
                        done = 0
                        for u in range(NQ + 2):
                            tiles = list(tiles_of(u)) if g is not None and u < NQ else []
                            if u < NQ:
                                scores(h, j, u, 0)
                            for t in tiles[:len(tiles) // 2]:
                                if t == 0:
                                    pe.wait_ge(loaded[1 - j], LOADS * (i + 1 + j))
                                tile(g, 1 - j, t)
                            if u < NQ:
                                scores(h, j, u, 1)
                            for t in tiles[len(tiles) // 2:]:
                                tile(g, 1 - j, t)
                            if 1 <= u <= NQ:
                                products(h, j, u - 1)
                            if g is not None and u == NQ - 4:
                                turn_negm(g, NCH * h + done)
                                pe.wait_ge(negm_copied, g + 1)
                            if u >= 2 and ends_tile(u - 2):
                                turn(h, u - 2)
                                done += 1

                    heads(pe, step)

        def stage_output(attn):
            scope = ExitStack()
            with scope:
                at_st = [sb(f"at_st{j}", [P, D], scope=scope) for j in range(2)]
                aT = [sb(f"aT{j}", [P, KD, P], scope=scope) for j in range(2)]
                xr = [sb(f"xr{j}", [P, D], scope=scope) for j in range(2)]
                yg = [[sb(f"yg{j}{k}", [P, D], scope=scope) for k in range(TOPK)] for j in range(2)]
                yidx = [[sb(f"yidx{j}{k}", [P, 1], I32, scope=scope) for k in range(TOPK)] for j in range(2)]
                sum0 = [sb(f"sum0{j}", [P, D], scope=scope) for j in range(2)]
                sum1 = [sb(f"sum1{j}", [P, D], scope=scope) for j in range(2)]
                res = [sb(f"res{j}", [P, D], scope=scope) for j in range(2)]
                psA = [scope.enter_context(nc.psum_tensor(f"psA{j}", [P, CH], F32)) for j in range(2)]
                psP = [scope.enter_context(nc.psum_tensor(f"psP{j}", [P, CH], F32)) for j in range(2)]
                staged, yidx_ready, y_here = sems("staged"), sems("yidx_ready"), sems("y_here")
                a_turned, aT_ready, projected = sems("a_turned"), sems("aT_ready"), sems("projected")
                xr_loaded, sums, res_ready, res_stored = sems("xr_loaded"), sems("sums"), sems("res_ready"), sems("res_stored")
                block = scope.enter_context(nc.Block())
                NI = NT // 2

                @block.sync
                def _(sp):
                    for j in (0, 1):
                        sp.dma_start(xr[j][:], x_rows[j * P:(j + 1) * P, :]).then_inc(xr_loaded[j], 16)
                    with sp.Fori(0, NI - 1) as i:
                        for j in (0, 1):
                            sp.wait_ge(res_ready[j], i + 1)
                            sp.dma_start(out_rows[bass.ds((2 * i + j) * P, P), :], res[j][:]).then_inc(res_stored[j], 16)
                            sp.dma_start(xr[j][:], x_rows[bass.ds((2 * i + j + 2) * P, P), :]).then_inc(xr_loaded[j], 16)
                    for j in (0, 1):
                        sp.wait_ge(res_ready[j], NI)
                        sp.dma_start(out_rows[(2 * NI - 2 + j) * P:(2 * NI - 1 + j) * P, :], res[j][:]).then_inc(res_stored[j], 16)
                    for j in (0, 1):
                        sp.wait_ge(res_stored[j], 16 * NI)

                @block.gpsimd
                def _(pool):
                    with pool.Fori(0, NI) as i:
                        for j in (0, 1):
                            pool.wait_ge(a_turned[j], i)
                            pool.tensor_copy(at_st[j][:], attn[:, bass.ds(2 * i + j, 1), :].rearrange("p b d -> p (b d)")).then_inc(staged[j], 1)
                            pool.wait_ge(y_here[j], 32 * i)
                            pool.wait_ge(sums[j], 2 * i)
                            for k in range(TOPK):
                                pool.tensor_copy(yidx[j][k][:], slot_in[:, k, bass.ds(2 * i + j, 1)]).then_inc(yidx_ready[j], 1)
                            for k in range(TOPK):
                                wait_apart(pool, "pool", yidx_ready[j], 2 * i + k + 1)
                                pool.indirect_dma_start(out=yg[j][k][:], out_offset=None, in_=y_dram,
                                                        in_offset=bass.IndirectOffsetOnAxis(ap=yidx[j][k][:, 0:1], axis=0),
                                                        bounds_check=NB * P - 1, oob_is_err=False).then_inc(y_here[j], 16)

                @block.scalar
                def _(act):
                    with act.Fori(0, NI) as i:
                        for j in (0, 1):
                            act.wait_ge(a_turned[j], i + 1)
                            act.wait_ge(projected[j], i)
                            act.copy(aT[j][:], psA[j][:, 0:D].rearrange("p (k t) -> p k t", k=KD)).then_inc(aT_ready[j], 1)

                @block.vector
                def _(dve):
                    with dve.Fori(0, NI) as i:
                        for j in (0, 1):
                            dve.wait_ge(xr_loaded[j], 16 * i + 16)
                            dve.wait_ge(y_here[j], 32 * i + 32)
                            dve.scalar_tensor_tensor(out=sum0[j][:], in0=yg[j][0][:], scalar=gates[:, 0, bass.ds(2 * i + j, 1)],
                                                     in1=xr[j][:], op0=ALU.mult, op1=ALU.add).then_inc(sums[j], 1)
                            dve.wait_ge(sums[j], 2 * i + 1)
                            dve.scalar_tensor_tensor(out=sum1[j][:], in0=yg[j][1][:], scalar=gates[:, 1, bass.ds(2 * i + j, 1)],
                                                     in1=sum0[j][:], op0=ALU.mult, op1=ALU.add).then_inc(sums[j], 1)
                            dve.wait_ge(sums[j], 2 * i + 2)
                            dve.wait_ge(projected[j], i + 1)
                            dve.wait_ge(res_stored[j], 16 * i)
                            dve.tensor_tensor(res[j][:], sum1[j][:], psP[j][:, 0:D], ALU.add).then_inc(res_ready[j], 1)

                @block.tensor
                def _(pe):
                    with pe.Fori(0, NI) as i:
                        for j in (0, 1):
                            pe.wait_ge(staged[j], i + 1)
                            pe.wait_ge(aT_ready[j], i)
                            for k in range(KD):
                                ins = pe.transpose(psA[j][:, k * P:(k + 1) * P], at_st[j][:, k * P:(k + 1) * P], ident)
                            ins.then_inc(a_turned[j], 1)
                            pe.wait_ge(aT_ready[j], i + 1)
                            pe.wait_ge(res_ready[j], i)
                            pe.matmul(psP[j][:, 0:D], ones[0:1, :], bp[:], start=True, stop=False)
                            for k in range(KD):
                                ins = pe.matmul(psP[j][:, 0:D], aT[j][:, k, :], wp[:, k, :], start=False, stop=(k == KD - 1))
                            ins.then_inc(projected[j], 1)

        stage_tokens()
        stage_queries()
        stage_experts()
        weights.close()
        with nc.sbuf_tensor("attn", [P, NT, D], F32) as attn_t:
            stage_attend(attn_t)
            stage_output(attn_t)


def kernel(L0_attn_hidden_states, L0_attn_c_attn_w, L0_attn_c_attn_b, L0_attn_c_proj_w, L0_attn_c_proj_b,
           L0_ffn_router_w, L0_ffn_w1, L0_ffn_w2):
    import concourse.bacc as bacc
    from concourse.bass_utils import run_bass_kernel_spmd

    nc = bacc.Bacc("TRN2", target_bir_lowering=False, num_devices=1)
    arrays = {
        "x": L0_attn_hidden_states, "w_attn": L0_attn_c_attn_w, "b_attn": np.asarray(L0_attn_c_attn_b)[None, :],
        "b_qk": np.asarray(L0_attn_c_attn_b)[:2 * D].reshape(4, P).T, "w_proj": L0_attn_c_proj_w, "b_proj": np.asarray(L0_attn_c_proj_b)[None, :],
        "w_router": np.asarray(L0_ffn_router_w).T, "w1": L0_ffn_w1, "w2": L0_ffn_w2, "consts": const_array(),
    }
    arrays = {n: np.ascontiguousarray(a) for n, a in arrays.items()}
    args = [nc.dram_tensor(n, a.shape, mybir.dt.from_np(a.dtype), kind="ExternalInput").ap() for n, a in arrays.items()]
    out = nc.dram_tensor("out", (1, S, D), F32, kind="ExternalOutput").ap()
    build(nc, *args, out)
    r = run_bass_kernel_spmd(nc, [arrays], core_ids=[0])
    return r.results[0]["out"]
```

```python
import numpy as np

import concourse.bass as bass
from concourse import mybir

P = 128
F32 = mybir.dt.float32
BF16 = mybir.dt.bfloat16
I32 = mybir.dt.int32
ALU = mybir.AluOpType
ACT = mybir.ActivationFunctionType
AX = mybir.AxisListType.X

S, D, H, HD = 4096, 256, 16, 16
E, F, CAP = 8, 1024, 1280
TOPK = 2
NT = S // P
CH = 512
NCH = S // CH
KD = D // P
KF = F // P
VW = HD + 1
NB = 72
JG = 20
NEG = -1.0e37
FAR = float(1 << 20)
EPS = 1e-5
SPLIT = 3
PAIRS = 6
AUG = PAIRS * HD + SPLIT
QUADS = [(qt, b) for qt in range(NCH - 1, -1, -1) for b in range(qt + 1)]
NQ = len(QUADS)
TILES = [(i, c) for c in range(NCH - 1, -1, -1) for i in range(4 * c, NT)]
NTL = len(TILES)
FIRST_EARLY = min(t for t, (i, c) in enumerate(TILES) if c < 2)
START = 1
CREDIT = 2
RING = 3


def const_layout():
    at, cols = {}, 0
    for name, width in (("ident", P), ("tri", P), ("sel", VW), ("mult", 3 * NT), ("eid", E), ("grid", JG),
                        ("block", NB), ("tok", NT), ("scan", TOPK * E * NT), ("maskT", 4 * P), ("maskS", P)):
        at[name] = (cols, width)
        cols += width
    return at, cols


def const_array():
    at, cols = const_layout()
    c = np.zeros((P, cols), np.float32)

    def put(name, value):
        a, w = at[name]
        c[:, a:a + w] = np.broadcast_to(value, (P, w))

    r = np.arange(P)
    put("ident", np.eye(P))
    put("tri", r[:, None] < r[None, :])
    sel = np.zeros((P, VW))
    for g in range(4):
        sel[32 * g + np.arange(VW), np.arange(VW)] = 1.0
    put("sel", sel)
    first, second = S // 3, 2 * S // 3
    pos = r[:, None] + P * np.arange(NT)[None, :]
    regions = [pos < first, (pos >= first) & (pos < second), pos >= second]
    put("mult", np.concatenate([np.float32(1.0) + np.float32(0.6) * g.astype(np.float32) for g in regions], 1))
    put("eid", np.arange(E) - E)
    put("grid", P * np.arange(JG))
    put("block", np.arange(NB))
    put("tok", pos)
    put("scan", (np.arange(TOPK * E * NT) % NT != 0))
    put("maskT", np.where(r[:, None] > np.arange(-3 * P, P)[None, :], NEG, 0.0))
    put("maskS", np.where(r[None, :] > r[:, None], NEG, 0.0))
    return c


def build(nc, x, w_attn, b_attn, b_qk, w_proj, b_proj, w_router, w1, w2, consts, out):
    at, CW = const_layout()
    from contextlib import ExitStack
    ctx = ExitStack()
    with ctx:
        def sb(name, shape, dt=F32, scope=ctx):
            return scope.enter_context(nc.sbuf_tensor(name, shape, dt))

        fresh = []

        def sem(name):
            fresh.append(ctx.enter_context(nc.semaphore(name)))
            return fresh[-1]

        def start_counts(pool):
            for s in fresh:
                pool.sem_inc(s, START)
            fresh.clear()

        def pool_dma_sems(name, n=2):
            return [ctx.enter_context(nc.semaphore(f"{name}{j}")) for j in range(n)]

        def sems(name, n=2):
            return [sem(f"{name}{j}") for j in range(n)]

        x_rows = x.rearrange("a s d -> (a s) d")
        out_rows = out.rearrange("a s d -> (a s) d")
        xn_dram = nc.dram_tensor("xn_scratch", [S, D], F32, kind="Internal").ap()
        qk_dram = nc.dram_tensor("qk_scratch", [2, SPLIT, D, S], BF16, kind="Internal").ap()
        list_dram = nc.dram_tensor("list_scratch", [NB * P, 1], F32, kind="Internal").ap()
        y_dram = nc.dram_tensor("y_scratch", [NB * P, D], F32, kind="Internal").ap()

        cst = sb("cst", [P, CW])

        def con(name):
            a, w = at[name]
            return cst[:, a:a + w]

        ident = con("ident")
        identb = sb("identb", [P, P], BF16)
        maskT = sb("maskT", [P, 4 * P], BF16)
        maskS = sb("maskS", [P, P], BF16)
        ones = sb("ones", [P, P])
        eps = sb("eps", [P, 1])
        wqk = sb("wqk", [P, KD, 2 * D])
        wv = sb("wv", [P, KD, D + E])
        bv = sb("bv", [P, D])
        bqk = sb("bqk", [P, 4])
        bqk4 = sb("bqk4", [P, 4])
        wp = sb("wp", [P, KD, D])
        bp = sb("bp", [P, D])
        v_all = sb("v_all", [P, H, NT, VW])
        logits = sb("logits", [P, NT, E])
        gates = sb("gates", [P, TOPK, NT])
        slot_out = sb("slot_out", [P, TOPK, NT], I32)
        slot_in = sb("slot_in", [P, TOPK, NT], I32)
        expert_of = sb("expert_of", [P, NB], I32)

        passed = {name: sem(f"passed_{name}") for name in ("sp", "pool", "dve")}

        def wait_apart(eng, name, semaphore, value):
            eng.wait_ge(semaphore, value)
            eng.sem_inc(passed[name], 1)

        s_const = sem("s_const")
        s_vec0 = sem("s_vec0")
        s_pool0 = sem("s_pool0")

        weights = ctx.enter_context(ExitStack())
        w1_sb = sb("w1_sb", [P, KD, E, F], scope=weights)
        w2_sb = sb("w2_sb", [P, E, KF, D], scope=weights)
        lent = w2_sb[:].rearrange("p e k d -> p (e k d)")
        xT_all = lent[:, E * F // 2 * KD:].rearrange("p (c x) -> p c x", c=NCH)
        half = 4 * D
        x_st = [lent[:, j * half:(j + 1) * half].rearrange("p (b d) -> p b d", b=4) for j in (0, 1)]
        xn_st = [lent[:, j * half:(j + 1) * half].rearrange("p (b d) -> p b d", b=4) for j in (2, 3)]
        xT_st = [lent[:, j * half:(j + 1) * half].rearrange("p (k s) -> p k s", k=KD) for j in (4, 5)]
        w1_dram = w1.rearrange("e (k p) f -> e p k f", p=P)
        w2_dram = w2.rearrange("e (k p) d -> e p k d", p=P)

        w1_loaded = sem("w1_loaded")
        w2_loaded = sem("w2_loaded")

        def stage_tokens():
            scope = ExitStack()
            with scope:
                stats = [sb(f"stats{j}", [P, 4, 6], scope=scope) for j in range(2)]
                mv = [sb(f"mv{j}", [P, 4, 2], scope=scope) for j in range(2)]
                std = [sb(f"std{j}", [P, 4], scope=scope) for j in range(2)]
                rstd = [sb(f"rstd{j}", [P, 4], scope=scope) for j in range(2)]
                psT = [scope.enter_context(nc.psum_tensor(f"psT{j}", [P, KD, CH], F32)) for j in range(2)]
                psV = scope.enter_context(nc.psum_tensor("psV", [P, 4, CH], F32))
                x_loaded = sems("x_loaded")
                st_ready, mv_ready, std_ready = sem("st_ready"), sems("mv_ready"), sems("std_ready")
                rstd_ready = sem("rstd_ready")
                xn_ready, xn_stored = sems("xn_ready"), sems("xn_stored")
                xT_in_psum, xT_ready, xT_kept = sems("xT_in_psum"), sems("xT_ready"), sems("xT_kept")
                v_in_psum, v_out = sem("v_in_psum"), sem("v_out")
                x_blocks = x_rows.rearrange("(c b p) d -> c p b d", p=P, b=4)
                xn_blocks = xn_dram.rearrange("(c b p) d -> c p b d", p=P, b=4)
                block = scope.enter_context(nc.Block())

                @block.sync
                def _(sp):
                    sp.dma_start(cst[:], consts).then_inc(s_const, 16)
                    sp.dma_start(wv[:, :, 0:D], w_attn[:, 2 * D:3 * D].rearrange("(k p) n -> p k n", p=P)).then_inc(s_const, 16)
                    sp.dma_start(wv[:, :, D:D + E], w_router.rearrange("(k p) e -> p k e", p=P)).then_inc(s_const, 16)
                    sp.dma_start(bv[:], b_attn[:, 2 * D:3 * D].to_broadcast([P, D])).then_inc(s_const, 16)
                    with sp.Fori(0, NCH // 2) as i:
                        for j in (0, 1):
                            sp.wait_ge(xn_ready[j], START + 4 * i)
                            sp.dma_start(x_st[j], x_blocks[bass.ds(2 * i + j, 1)].rearrange("c p b d -> (c p) b d")).then_inc(x_loaded[j], 16)
                            sp.dma_start(w1_sb[:, :, bass.ds(2 * i + j, 1), :].rearrange("p k e f -> p (k e) f"),
                                         w1_dram[bass.ds(2 * i + j, 1)].rearrange("e p k f -> (e p) k f")).then_inc(w1_loaded, 16)
                    sp.dma_start(wqk[:], w_attn[:, 0:2 * D].rearrange("(k p) n -> p k n", p=P)).then_inc(s_const, 16)
                    sp.dma_start(bqk[:], b_qk).then_inc(s_const, 16)
                    sp.dma_start(wp[:], w_proj.rearrange("(k p) n -> p k n", p=P)).then_inc(s_const, 16)
                    sp.dma_start(bp[:], b_proj.to_broadcast([P, D])).then_inc(s_const, 16)

                @block.gpsimd
                def _(pool):
                    start_counts(pool)
                    pool.memset(ones[:], 1.0).then_inc(s_pool0, 1)
                    pool.memset(eps[:], EPS).then_inc(s_pool0, 1)
                    pool.memset(v_all[:, :, :, HD:VW], 1.0).then_inc(s_pool0, 1)
                    with pool.Fori(0, NCH // 2) as i:
                        for j in (0, 1):
                            pool.wait_ge(xT_ready[j], START + 2 * i + 2)
                            pool.tensor_copy(xT_all[:, bass.ds(2 * i + j, 1), :].rearrange("p c x -> p (c x)"),
                                             xT_st[j].rearrange("p k s -> p (k s)")).then_inc(xT_kept[j], 1)

                def chunks(eng, first, both, last):
                    first()
                    with eng.Fori(0, NCH // 2 - 1) as i:
                        both(2 * i, i, 0)
                        both(2 * i + 1, i, 1)
                    both(NCH - 2, NCH // 2 - 1, 0)
                    last(NCH - 1, NCH // 2 - 1, 1)

                @block.vector
                def _(dve):
                    dve.wait_ge(s_const, START + 64)
                    dve.tensor_copy(identb[:], ident).then_inc(s_vec0, 1)
                    dve.tensor_copy(maskT[:], con("maskT")).then_inc(s_vec0, 1)
                    dve.tensor_copy(maskS[:], con("maskS")).then_inc(s_vec0, 1)

                    def normalize(n, i, j):
                        dve.wait_ge(x_loaded[j], START + 16 * i + 16)
                        for b in range(4):
                            dve.bn_stats(stats[j][:, b, :], x_st[j][:, b, :]).then_inc(st_ready, 1)
                        wait_apart(dve, "dve", st_ready, START + 4 * n + 4)
                        for b in range(4):
                            dve.bn_aggr(mv[j][:, b, :], stats[j][:, b, :]).then_inc(mv_ready[j], 1)
                        dve.wait_ge(std_ready[j], START + i + 1)
                        dve.reciprocal(rstd[j][:], std[j][:]).then_inc(rstd_ready, 1)
                        dve.wait_ge(rstd_ready, START + n + 1)
                        dve.wait_ge(xT_in_psum[j], START + i)
                        dve.wait_ge(xn_stored[j], START + 16 * i)
                        for b in range(4):
                            dve.tensor_scalar(xn_st[j][:, b, :], x_st[j][:, b, :], mv[j][:, b, 0:1],
                                              rstd[j][:, b:b + 1], ALU.subtract, ALU.mult).then_inc(xn_ready[j], 1)

                    def keep_turned(n, i, j):
                        dve.wait_ge(xT_in_psum[j], START + i + 1)
                        dve.wait_ge(xT_kept[j], START + i)
                        dve.wait_ge(v_in_psum, START + 2 * i)
                        dve.tensor_copy(xT_st[j][:, 1, :], psT[j][:, 1, :]).then_inc(xT_ready[j], 1)

                    def keep_values(n, i, j):
                        dve.wait_ge(v_in_psum, START + n + 1)
                        for b in range(4):
                            dve.tensor_tensor(v_all[:, :, bass.ds(4 * n + b, 1), 0:HD].rearrange("p h b d -> p h (b d)"),
                                              psV[:, b, 0:D].rearrange("p (h d) -> p h d", h=H),
                                              bv[:].rearrange("p (h d) -> p h d", h=H), ALU.add)
                        dve.tensor_copy(logits[:, bass.ds(4 * n, 4), :], psV[:, :, D:D + E]).then_inc(v_out, 1)

                    def both(n, i, j):
                        keep_turned(n, i, j)
                        normalize(n + 1, i + j, 1 - j)
                        keep_values(n, i, j)

                    def last(n, i, j):
                        keep_turned(n, i, j)
                        keep_values(n, i, j)

                    chunks(dve, lambda: normalize(0, 0, 0), both, last)

                @block.scalar
                def _(act):
                    act.wait_ge(s_pool0, START + 3)

                    def normalize(n, i, j):
                        act.wait_ge(mv_ready[j], START + 4 * i + 4)
                        act.wait_ge(rstd_ready, START + 2 * i)
                        act.activation(std[j][:], mv[j][:, :, 1], ACT.Sqrt, bias=eps[:, 0:1], scale=1.0).then_inc(std_ready[j], 1)
                        act.wait_ge(xn_ready[j], START + 4 * i + 4)
                        act.dma_start(xn_blocks[bass.ds(n, 1)].rearrange("c p b d -> (c p) b d"), xn_st[j]).then_inc(xn_stored[j], 16)

                    def keep_turned(n, i, j):
                        act.wait_ge(xT_in_psum[j], START + i + 1)
                        act.wait_ge(xT_kept[j], START + i)
                        act.wait_ge(v_in_psum, START + 2 * i)
                        act.copy(xT_st[j][:, 0, :], psT[j][:, 0, :]).then_inc(xT_ready[j], 1)

                    def both(n, i, j):
                        keep_turned(n, i, j)
                        normalize(n + 1, i + j, 1 - j)

                    chunks(act, lambda: normalize(0, 0, 0), both, keep_turned)
                    for j in (0, 1):
                        act.wait_ge(xn_stored[j], START + 16 * (NCH // 2))

                @block.tensor
                def _(pe):
                    pe.wait_ge(s_const, START + 64)

                    def turn(n, i, j):
                        pe.wait_ge(xn_ready[j], START + 4 * i + 4)
                        pe.wait_ge(xT_ready[j], START + 2 * i)
                        for k in range(KD):
                            for b in range(4):
                                ins = pe.transpose(psT[j][:, k, b * P:(b + 1) * P], xn_st[j][:, b, k * P:(k + 1) * P], ident)
                        ins.then_inc(xT_in_psum[j], 1)

                    def values(n, i, j):
                        pe.wait_ge(xT_ready[j], START + 2 * i + 2)
                        pe.wait_ge(v_out, START + n)
                        for b in range(4):
                            for k in range(KD):
                                ins = pe.matmul(psV[:, b, 0:D + E], xT_st[j][:, k, b * P:(b + 1) * P], wv[:, k, :],
                                                start=(k == 0), stop=(k == KD - 1))
                        ins.then_inc(v_in_psum, 1)

                    def both(n, i, j):
                        values(n, i, j)
                        turn(n + 1, i + j, 1 - j)

                    chunks(pe, lambda: turn(0, 0, 0), both, values)

        def stage_queries():
            scope = ExitStack()
            with scope:
                t_st = [sb(f"t_st{q}", [P, CH], scope=scope) for q in range(2)]
                r_both = sb("r_both", [P, 2 * CH], scope=scope)
                r_st = [r_both[:, q * CH:(q + 1) * CH] for q in range(2)]
                s_st = [sb(f"s_st{q}", [P, SPLIT, CH], BF16, scope=scope) for q in range(2)]
                big = TOPK * NT * E
                onehot = sb("onehot", [P, TOPK, NT, E], scope=scope)
                tmp = sb("tmp", [P, TOPK, NT, E], scope=scope)
                cnt = sb("cnt", [P, TOPK, E, NT], scope=scope)
                inc = sb("inc", [P, TOPK, E, NT], scope=scope)
                m1 = sb("m1", [P, NT], scope=scope)
                m2 = sb("m2", [P, NT], scope=scope)
                fst = sb("fst", [P, NT], scope=scope)
                e2 = sb("e2", [P, NT], scope=scope)
                pos = sb("pos", [P, TOPK, NT], scope=scope)
                keep = sb("keep", [P, TOPK, NT], scope=scope)
                tot = sb("tot", [P, TOPK, E], scope=scope)
                nsum = sb("nsum", [P, E], scope=scope)
                nblk = sb("nblk", [P, E], scope=scope)
                endb = sb("endb", [P, E], scope=scope)
                base = sb("base", [P, TOPK, E], scope=scope)
                blk = r_both[:, 0:NB * E].rearrange("p (b e) -> p b e", e=E)
                eidf = sb("eidf", [P, NB], scope=scope)
                zero = sb("zero", [NB, P], scope=scope)
                sidx = [sb(f"sidx{k}", [P, 1], I32, scope=scope) for k in range(TOPK)]
                stok = [sb(f"stok{k}", [P, 1], scope=scope) for k in range(TOPK)]
                psQ = [scope.enter_context(nc.psum_tensor(f"psQ{q}", [P, CH], F32)) for q in range(2)]
                psR = [scope.enter_context(nc.psum_tensor(f"psR{q}", [P, TOPK, NT, E], F32)) for q in range(2)]
                q_in_psum, t_ready, s1_ready = sems("q_in_psum"), sems("t_ready"), sems("s1_ready")
                r_ready, s2_ready, s3_ready, q_stored = sems("r_ready"), sems("s2_ready"), sems("s3_ready"), sems("q_stored")
                counted, gap_ready, e2_ready = sem("counted"), sem("gap_ready"), sem("e2_ready")
                ONEHOT_LINKS = 11
                slots_ready, zero_ready, listed = sem("slots_ready"), sem("zero_ready"), pool_dma_sems("listed")
                idx_ready, route = sem("idx_ready"), sem("route")
                list_zeroed = sem("list_zeroed")
                units = [(fc, fc % 2, fc // 2) for fc in range(4)]
                block = scope.enter_context(nc.Block())

                @block.sync
                def _(sp):
                    for e in range(E // 2):
                        sp.dma_start(w2_sb[:, e], w2_dram[e]).then_inc(w2_loaded, 16)
                    sp.wait_ge(zero_ready, START + 1)
                    sp.dma_start(list_dram.rearrange("(b p) o -> b (p o)", p=P), zero[:]).then_inc(list_zeroed, 16)
                    with sp.Fori(0, NCH // 2) as m:
                        for i in (2 * m, 2 * m + 1):
                            for fc, q, r in units:
                                sp.wait_ge(s3_ready[q], START + 2 * i + r + 1)
                                dst = qk_dram[fc // 2, :, (fc % 2) * P:(fc % 2 + 1) * P, bass.ds(i * CH, CH)]
                                sp.dma_start(dst.rearrange("c p s -> p c s"), s_st[q][:]).then_inc(q_stored[q], 16)
                        sp.dma_start(w2_sb[:, bass.ds(E // 2 + m, 1)].rearrange("p e k d -> p (e k) d"),
                                     w2_dram[bass.ds(E // 2 + m, 1)].rearrange("e p k d -> (e p) k d")).then_inc(w2_loaded, 16)
                    for q in range(2):
                        sp.wait_ge(q_stored[q], START + 16 * 2 * NCH)

                @block.gpsimd
                def _(pool):
                    start_counts(pool)
                    pool.memset(zero[:], 0.0).then_inc(zero_ready, 1)
                    pool.wait_ge(list_zeroed, START + 16)
                    pool.wait_ge(slots_ready, START + 2)

                    def scatter(i, first=False):
                        for k in range(TOPK):
                            if not first:
                                pool.wait_ge(listed[k], 16 * i)
                            pool.tensor_copy(sidx[k][:], slot_out[:, k, bass.ds(i, 1)]).then_inc(idx_ready, 1)
                            pool.tensor_copy(stok[k][:], con("tok")[:, bass.ds(i, 1)]).then_inc(idx_ready, 1)
                            wait_apart(pool, "pool", idx_ready, START + 4 * i + 2 * k + 2)
                            pool.indirect_dma_start(out=list_dram, out_offset=bass.IndirectOffsetOnAxis(ap=sidx[k][:, 0:1], axis=0),
                                                    in_=stok[k][:], in_offset=None, bounds_check=NB * P - 1,
                                                    oob_is_err=False).then_inc(listed[k], 16)

                    scatter(0, first=True)
                    with pool.Fori(1, NT) as i:
                        scatter(i)
                    for k in range(TOPK):
                        pool.wait_ge(listed[k], 16 * NT)

                @block.scalar
                def _(act):
                    act.wait_ge(s_const, START + 128)
                    act.mul(bqk4[:, 0:2], bqk[:, 0:2], 0.25)
                    act.copy(bqk4[:, 2:4], bqk[:, 2:4]).then_inc(s_vec0, 1)
                    act.wait_ge(s_vec0, START + 4)
                    act.wait_ge(gap_ready, START + 1)
                    act.activation(e2[:], e2[:], ACT.Exp).then_inc(e2_ready, 1)
                    with act.Fori(0, NCH) as i:
                        for fc, q, r in units:
                            act.wait_ge(q_in_psum[q], START + 2 * i + r + 1)
                            act.wait_ge(r_ready[q], START + 2 * i + r)
                            act.activation(t_st[q][:], psQ[q][:], ACT.Identity, bias=bqk4[:, fc:fc + 1],
                                           scale=0.25 if fc < 2 else 1.0).then_inc(t_ready[q], 1)
                            act.wait_ge(t_ready[q], START + 2 * i + r + 1)
                            act.wait_ge(q_stored[q], START + 32 * i + 16 * r)
                            act.copy(s_st[q][:, 0, :], t_st[q][:]).then_inc(s1_ready[q], 1)

                @block.vector
                def _(dve):
                    n = [0]

                    def link(ins):
                        n[0] += 1
                        ins.then_inc(route, 1)
                        dve.wait_ge(route, START + n[0])

                    def wide(a, shape):
                        return a.to_broadcast(shape)

                    eid = con("eid")
                    SH = [P, NT, E]
                    lg = logits[:]
                    for k, m in ((0, m1), (1, m2)):
                        link(dve.tensor_reduce(m[:], lg, AX, ALU.max))
                        link(dve.tensor_tensor(tmp[:, 0], lg, wide(m[:].unsqueeze(2), SH), ALU.is_equal))
                        link(dve.tensor_tensor(tmp[:, 0], tmp[:, 0], wide(eid.unsqueeze(1), SH), ALU.mult))
                        link(dve.tensor_reduce(fst[:], tmp[:, 0], AX, ALU.min))
                        link(dve.tensor_tensor(onehot[:, k], wide(eid.unsqueeze(1), SH), wide(fst[:].unsqueeze(2), SH), ALU.is_equal))
                        if k == 0:
                            link(dve.scalar_tensor_tensor(out=tmp[:, 1], in0=onehot[:, 0], scalar=-3.0e38, in1=lg,
                                                          op0=ALU.mult, op1=ALU.add))
                            lg = tmp[:, 1]
                    dve.tensor_tensor(e2[:], m2[:], m1[:], ALU.subtract).then_inc(gap_ready, 1)
                    assert n[0] == ONEHOT_LINKS
                    dve.wait_ge(e2_ready, START + 1)
                    link(dve.tensor_scalar(m1[:], e2[:], 1.0, None, ALU.add))
                    link(dve.reciprocal(gates[:, 0], m1[:]))
                    link(dve.tensor_tensor(gates[:, 1], e2[:], gates[:, 0], ALU.mult))
                    dve.wait_ge(counted, START + 2)
                    link(dve.tensor_copy(cnt[:].rearrange("p k e b -> p k b e"), psR[1][:]))
                    f = "p k e b -> p (k e b)"
                    link(dve.tensor_tensor_scan(inc[:].rearrange(f), con("scan"), cnt[:].rearrange(f), 0.0, ALU.mult, ALU.add))
                    link(dve.tensor_scalar(tot[:], inc[:, :, :, NT - 1], float(CAP), None, ALU.min))
                    link(dve.tensor_tensor(inc[:], inc[:], cnt[:], ALU.subtract))
                    for k in range(TOPK):
                        link(dve.tensor_tensor(tmp[:, k], inc[:, k].rearrange("p e b -> p b e"), psR[0][:, k], ALU.add))
                        link(dve.tensor_tensor(tmp[:, k], tmp[:, k], onehot[:, k], ALU.mult))
                        link(dve.tensor_reduce(pos[:, k], tmp[:, k], AX, ALU.add))
                    link(dve.tensor_tensor(nsum[:], tot[:, 0], tot[:, 1], ALU.add))
                    link(dve.tensor_tensor(tmp[:].rearrange("p k b e -> p (k b e)")[:, 0:E * JG].rearrange("p (e j) -> p e j", e=E),
                                           wide(nsum[:].unsqueeze(2), [P, E, JG]), wide(con("grid").unsqueeze(1), [P, E, JG]), ALU.is_gt))
                    link(dve.tensor_reduce(nblk[:], tmp[:].rearrange("p k b e -> p (k b e)")[:, 0:E * JG].rearrange("p (e j) -> p e j", e=E),
                                           AX, ALU.add))
                    link(dve.tensor_tensor_scan(endb[:], ones[:, 0:E], nblk[:], 0.0, ALU.mult, ALU.add))
                    link(dve.tensor_tensor(base[:, 0], endb[:], nblk[:], ALU.subtract))
                    link(dve.tensor_scalar(base[:, 0], base[:, 0], float(P), None, ALU.mult))
                    link(dve.tensor_tensor(base[:, 1], base[:, 0], tot[:, 0], ALU.add))
                    link(dve.tensor_scalar(keep[:], pos[:], float(CAP), None, ALU.is_lt))
                    for k in range(TOPK):
                        link(dve.tensor_tensor(tmp[:, k], onehot[:, k], wide(base[:, k].unsqueeze(1), SH), ALU.mult))
                        link(dve.tensor_reduce(m1[:], tmp[:, k], AX, ALU.add))
                        link(dve.tensor_tensor(pos[:, k], pos[:, k], m1[:], ALU.add))
                    link(dve.tensor_tensor(gates[:], gates[:], keep[:], ALU.mult))
                    link(dve.tensor_tensor(pos[:], pos[:], keep[:], ALU.mult))
                    dve.tensor_copy(slot_in[:], pos[:]).then_inc(slots_ready, 1)
                    link(dve.tensor_scalar(keep[:], keep[:], -FAR, FAR, ALU.mult, ALU.add))
                    link(dve.tensor_tensor(pos[:], pos[:], keep[:], ALU.add))
                    dve.tensor_copy(slot_out[:], pos[:]).then_inc(slots_ready, 1)
                    link(dve.tensor_tensor(blk, wide(endb[:].unsqueeze(1), [P, NB, E]), wide(con("block").unsqueeze(2), [P, NB, E]), ALU.is_le))
                    link(dve.tensor_reduce(eidf[:], blk, AX, ALU.add))
                    link(dve.tensor_scalar(eidf[:], eidf[:], float(E - 1), None, ALU.min))
                    link(dve.tensor_copy(expert_of[:], eidf[:]))
                    dve.wait_ge(s_pool0, START + 3)
                    for h in range(3):
                        dve.tensor_tensor(v_all[:, h], v_all[:, h],
                                          wide(con("mult")[:, h * NT:(h + 1) * NT].unsqueeze(2), [P, NT, VW]), ALU.mult)
                    with dve.Fori(0, NCH) as i:
                        for fc, q, r in units:
                            dve.wait_ge(s1_ready[q], START + 2 * i + r + 1)
                            dve.tensor_tensor(r_st[q], t_st[q][:], s_st[q][:, 0, :], ALU.subtract).then_inc(r_ready[q], 1)
                            dve.wait_ge(r_ready[q], START + 2 * i + r + 1)
                            dve.tensor_copy(s_st[q][:, 1, :], r_st[q]).then_inc(s2_ready[q], 1)
                            dve.wait_ge(s2_ready[q], START + 2 * i + r + 1)
                            dve.tensor_tensor(s_st[q][:, 2, :], r_st[q], s_st[q][:, 1, :], ALU.subtract).then_inc(s3_ready[q], 1)

                @block.tensor
                def _(pe):
                    pe.wait_ge(s_const, START + 128)

                    def count():
                        pe.wait_ge(route, START + ONEHOT_LINKS)
                        rows = onehot[:].rearrange("p k b e -> p (k b e)")
                        pe.matmul(psR[0][:].rearrange("p k b e -> p (k b e)"), con("tri"), rows, start=True, stop=True).then_inc(counted, 1)
                        pe.matmul(psR[1][:].rearrange("p k b e -> p (k b e)"), ones[:], rows, start=True, stop=True).then_inc(counted, 1)

                    count()
                    with pe.Fori(0, NCH) as i:
                        for fc, q, r in units:
                            pe.wait_ge(t_ready[q], START + 2 * i + r)
                            for k in range(KD):
                                ins = pe.matmul(psQ[q][:], wqk[:, k, fc * P:(fc + 1) * P], xT_all[:, bass.ds(i, 1), k * CH:(k + 1) * CH].rearrange("p c s -> p (c s)"),
                                                start=(k == 0), stop=(k == KD - 1))
                            ins.then_inc(q_in_psum[q], 1)

        def stage_experts():
            scope = ExitStack()
            with scope:
                listed_rows = sb("listed_rows", [NB, P], scope=scope)
                tokens = sb("tokens", [P, NB], I32, scope=scope)
                gidx = [sb(f"gidx{j}", [P, 1], I32, scope=scope) for j in range(2)]
                xg = [sb(f"xg{j}", [P, D], scope=scope) for j in range(2)]
                xgT = [sb(f"xgT{j}", [P, KD, P], scope=scope) for j in range(2)]
                h_sb = sb("h_sb", [P, F], scope=scope)
                hT = sb("hT", [P, KF, P], scope=scope)
                y_sb = [sb(f"y_sb{j}", [P, D], scope=scope) for j in range(2)]
                psX = scope.enter_context(nc.psum_tensor("psX", [P, CH], F32))
                psH = scope.enter_context(nc.psum_tensor("psH", [P, F], F32))
                psHT = scope.enter_context(nc.psum_tensor("psHT", [P, KF, P], F32))
                psY = [scope.enter_context(nc.psum_tensor(f"psY{j}", [P, CH], F32)) for j in range(2)]
                list_loaded, list_turned, tokens_ready = sem("list_loaded"), sem("list_turned"), sem("tokens_ready")
                gidx_ready, gathered = sems("gidx_ready"), pool_dma_sems("gathered")
                x_turned, xgT_ready = sem("x_turned"), sem("xgT_ready")
                h_in_psum, h_ready, h_turned, hT_ready = sem("h_in_psum"), sem("h_ready"), sem("h_turned"), sem("hT_ready")
                y_in_psum, y_ready, y_stored = sem("y_in_psum"), sem("y_ready"), sems("y_stored")
                block = scope.enter_context(nc.Block())
                NI = NB // 2

                @block.sync
                def _(sp):
                    sp.dma_start(listed_rows[:], list_dram.rearrange("(b p) o -> b (p o)", p=P)).then_inc(list_loaded, 16)
                    with sp.Fori(0, NI) as i:
                        for j in (0, 1):
                            sp.wait_ge(y_ready, START + 2 * i + j + 1)
                            sp.dma_start(y_dram[bass.ds((2 * i + j) * P, P), :], y_sb[j][:]).then_inc(y_stored[j], 16)
                    for j in (0, 1):
                        sp.wait_ge(y_stored[j], START + 16 * NI)

                @block.gpsimd
                def _(pool):
                    start_counts(pool)
                    pool.wait_ge(tokens_ready, START + 1)

                    def gather(i, first=False):
                        for j in (0, 1):
                            if not first:
                                pool.wait_ge(x_turned, START + 2 * i - 1 + j)
                                pool.wait_ge(gathered[j], 16 * i)
                            pool.tensor_copy(gidx[j][:], tokens[:, bass.ds(2 * i + j, 1)]).then_inc(gidx_ready[j], 1)
                            wait_apart(pool, "pool", gidx_ready[j], START + i + 1)
                            pool.indirect_dma_start(out=xg[j][:], out_offset=None, in_=xn_dram,
                                                    in_offset=bass.IndirectOffsetOnAxis(ap=gidx[j][:, 0:1], axis=0),
                                                    bounds_check=S - 1, oob_is_err=False).then_inc(gathered[j], 16)

                    gather(0, first=True)
                    with pool.Fori(1, NI) as i:
                        gather(i)

                @block.vector
                def _(dve):
                    dve.wait_ge(list_turned, START + 1)
                    dve.tensor_copy(tokens[:], psX[:, 0:NB]).then_inc(tokens_ready, 1)

                    def x_copy(n, j):
                        dve.wait_ge(x_turned, START + n + 1)
                        dve.tensor_copy(xgT[j][:], psX[:, 0:D].rearrange("p (k t) -> p k t", k=KD)).then_inc(xgT_ready, 1)

                    x_copy(0, 0)
                    x_copy(1, 1)
                    with dve.Fori(0, NI - 1) as i:
                        for j in (0, 1):
                            dve.wait_ge(h_turned, START + 2 * i + j + 1)
                            dve.tensor_copy(hT[:], psHT[:]).then_inc(hT_ready, 1)
                            dve.wait_ge(h_in_psum, START + 2 * i + j + 1)
                            x_copy(2 * i + j + 2, j)
                    for n in (NB - 2, NB - 1):
                        dve.wait_ge(h_turned, START + n + 1)
                        dve.tensor_copy(hT[:], psHT[:]).then_inc(hT_ready, 1)

                @block.scalar
                def _(act):
                    def gelu(n):
                        act.wait_ge(h_in_psum, START + n + 1)
                        act.wait_ge(h_turned, START + n)
                        act.activation(h_sb[:], psH[:], ACT.Gelu).then_inc(h_ready, 1)

                    def y_copy(n, i, j):
                        act.wait_ge(y_in_psum, START + n + 1)
                        act.wait_ge(y_stored[j], START + 16 * i)
                        act.copy(y_sb[j][:], psY[j][:, 0:D]).then_inc(y_ready, 1)

                    gelu(0)
                    with act.Fori(0, NI - 1) as i:
                        for j in (0, 1):
                            gelu(2 * i + j + 1)
                            y_copy(2 * i + j, i, j)
                    gelu(NB - 1)
                    y_copy(NB - 2, NI - 1, 0)
                    y_copy(NB - 1, NI - 1, 1)

                @block.tensor
                def _(pe):
                    pe.wait_ge(list_loaded, START + 16)
                    pe.transpose(psX[:, 0:NB], listed_rows[:], ident[0:NB, 0:NB]).then_inc(list_turned, 1)
                    pe.wait_ge(tokens_ready, START + 1)

                    def turn_x(n, i, j):
                        pe.wait_ge(gathered[j], 16 * i + 16)
                        pe.wait_ge(xgT_ready, START + n)
                        for k in range(KD):
                            ins = pe.transpose(psX[:, k * P:(k + 1) * P], xg[j][:, k * P:(k + 1) * P], ident)
                        ins.then_inc(x_turned, 1)

                    def first(n, j):
                        expert = pe.value_load(expert_of[0:1, bass.ds(n, 1)], min_val=0, max_val=E - 1)
                        pe.wait_ge(xgT_ready, START + n + 1)
                        pe.wait_ge(h_ready, START + n)
                        for k in range(KD):
                            for c in range(F // CH):
                                ins = pe.matmul(psH[:, c * CH:(c + 1) * CH], xgT[j][:, k, :],
                                                w1_sb[:, k, bass.ds(expert, 1), c * CH:(c + 1) * CH].rearrange("p e f -> p (e f)"),
                                                start=(k == 0), stop=(k == KD - 1))
                        ins.then_inc(h_in_psum, 1)

                    def turn_h(n):
                        pe.wait_ge(h_ready, START + n + 1)
                        pe.wait_ge(hT_ready, START + n)
                        for k in range(KF):
                            ins = pe.transpose(psHT[:, k, :], h_sb[:, k * P:(k + 1) * P], ident)
                        ins.then_inc(h_turned, 1)

                    def second(n, i, j):
                        expert = pe.value_load(expert_of[0:1, bass.ds(n, 1)], min_val=0, max_val=E - 1)
                        pe.wait_ge(hT_ready, START + n + 1)
                        if j == 0:
                            pe.wait_ge(y_ready, START + 2 * i)
                        else:
                            pe.wait_ge(y_ready, START + 2 * i)
                        for k in range(KF):
                            ins = pe.matmul(psY[j][:, 0:D], hT[:, k, :],
                                            w2_sb[:, bass.ds(expert, 1), k, :].rearrange("p e d -> p (e d)"),
                                            start=(k == 0), stop=(k == KF - 1))
                        ins.then_inc(y_in_psum, 1)

                    turn_x(0, 0, 0)
                    pe.wait_ge(w1_loaded, START + 16 * E)
                    first(0, 0)
                    turn_x(1, 0, 1)
                    pe.wait_ge(w2_loaded, START + 16 * E)
                    with pe.Fori(0, NI - 1) as i:
                        for j in (0, 1):
                            turn_h(2 * i + j)
                            first(2 * i + j + 1, 1 - j)
                            second(2 * i + j, i, j)
                            turn_x(2 * i + j + 2, i + 1, j)
                    turn_h(NB - 2)
                    first(NB - 1, 1)
                    second(NB - 2, NI - 1, 0)
                    turn_h(NB - 1)
                    second(NB - 1, NI - 1, 1)

        def stage_attend(attn, side):
            scope = ExitStack()
            with scope:
                qa = [sb(f"qa{j}", [AUG, S], BF16, scope=scope) for j in range(2)]
                ka = [sb(f"ka{j}", [AUG, S], BF16, scope=scope) for j in range(2)]
                vh = [sb(f"vh{j}", [P, NT, 32], scope=scope) for j in range(2)]
                probs = [sb(f"probs{j}", [P, 4, CH], scope=scope) for j in range(2)]
                oT = [sb(f"oT{j}", [P, CH], scope=scope) for j in range(2)]
                rden = sb("rden", [P, 4, 1], scope=scope)
                mxp = sb("mxp", [P, NT, NCH], scope=scope)
                nm = sb("nm", [P, NT], scope=scope)
                nr = sb("nr", [P, NT], scope=scope)
                nm3 = sb("nm3", [P, SPLIT, NT], BF16, scope=scope)
                mT = sb("mT", [SPLIT * NT, P], BF16, scope=scope)
                psS = scope.enter_context(nc.psum_tensor("psS", [P, RING, CH], F32))
                psM = scope.enter_context(nc.psum_tensor("psM", [P, RING, CH], F32))
                psO = scope.enter_context(nc.psum_tensor("psO", [P, CH], F32))
                psN = scope.enter_context(nc.psum_tensor("psN", [P, CH], F32))
                psMT = psN[:].bitcast(BF16)[0:SPLIT * NT, CH:CH + P]
                aug_ones, pads = sem("aug_ones"), sem("pads")
                late_loaded, early_loaded = sems("late_loaded"), sems("early_loaded")
                v_ready = sem("v_ready")
                s_ready, exp_done, pv_done = sem("s_ready"), sem("exp_done"), sem("pv_done")
                o_copied, o_turned, normed, recip = sem("o_copied"), sem("o_turned"), sem("normed"), sem("recip")
                m_ready, m_done, m_chain = sem("m_ready"), sem("m_done"), sem("m_chain")
                negm_ready, negm_turned, negm_copied, negm_loaded = (
                    sem("negm_ready"), sem("negm_turned"), sem("negm_copied"), sem("negm_loaded"))
                yg = [sb(f"yg{k}", [P, D], scope=scope) for k in range(TOPK)]
                xr = sb("xr", [P, D], scope=scope)
                yidx = [sb(f"yidx{k}", [P, 1], I32, scope=scope) for k in range(TOPK)]
                ygate = [sb(f"ygate{k}", [P, 1], scope=scope) for k in range(TOPK)]
                (y_here, xr_here), side_step = pool_dma_sems("side_rows"), sem("side_step")
                SIDE_STEPS = 9
                M_LINKS = 6
                NI = H // 2 - 1
                LATE, EARLY = 3 * 6 * 16, 6 * 16
                block = scope.enter_context(nc.Block())

                def heads(eng, step):
                    with eng.Fori(0, NI) as i:
                        step(2 * i, 0, 2 * i + 1, i)
                        step(2 * i + 1, 1, 2 * i + 2, i)
                    step(H - 2, 0, H - 1, NI)
                    step(H - 1, 1, None, NI)

                def tiles_of(u):
                    n = NQ - 3
                    return range(NTL * min(u, n) // n, NTL * min(u + 1, n) // n)

                def ends_tile(u):
                    return u == NQ - 1 or QUADS[u + 1][0] != QUADS[u][0]

                def places(u):
                    qt, b = QUADS[u]
                    if b < qt or qt == 0:
                        return [(g, 0, CH) for g in range(4)]
                    return [(0, 0, CH), (1, 0, 3 * P), (2, 0, 2 * P), (2, 2 * P, P)]

                widths = [[sum(w for n, _, w in places(u) if n == m) for m in range(places(u)[3][0] + 1)] for u in range(NQ)]
                first_unit = [sum(len(w) for w in widths[:u]) for u in range(NQ + 1)]
                NU = first_unit[NQ]

                def before(n):
                    return n - RING if n >= RING else max(m for m in range(NU) if m % RING == n) - NU

                @block.sync
                def _(sp):
                    def load(g, j, step):
                        cols = slice((3 - step) * 2 * CH, (4 - step) * 2 * CH)
                        f = bass.ds(g * HD, HD)
                        loaded = early_loaded if step == 3 else late_loaded
                        r = 0
                        for which in range(SPLIT):
                            n = SPLIT - which
                            sp.dma_start(qa[j][r:r + n * HD, cols], qk_dram[0, 0:n, f, cols]).then_inc(loaded[j], 16)
                            sp.dma_start(ka[j][r:r + n * HD, cols],
                                         qk_dram[1, which:which + 1, f, cols].to_broadcast([n, HD, 2 * CH])).then_inc(loaded[j], 16)
                            r += n * HD

                    def negm(g, j):
                        sp.wait_ge(negm_copied, START + g + 1)
                        for c in range(SPLIT):
                            sp.dma_start(qa[j][PAIRS * HD + c:PAIRS * HD + c + 1, :].rearrange("c (b q) -> c b q", q=P),
                                         mT[c * NT:(c + 1) * NT, :]).then_inc(negm_loaded, 16)

                    for g in (0, 1):
                        for step in range(4):
                            load(g, g, step)
                    negm(0, 0)

                    def step(h, j, g, i):
                        for part in range(4):
                            last = max(u for u in range(NQ) if QUADS[u][0] == 6 - 2 * part)
                            if g is not None and not isinstance(g, int):
                                wait_apart(sp, "sp", pv_done, START + NQ * h + last + 1 + CREDIT)
                                load(h + 2, j, part)
                            if part == 2 and g is not None:
                                negm(g, 1 - j)

                    heads(sp, step)

                @block.gpsimd
                def _(pool):
                    start_counts(pool)
                    for j in (0, 1):
                        pool.memset(ka[j][PAIRS * HD:AUG, :], 1.0).then_inc(aug_ones, 1)
                    pool.wait_ge(aug_ones, START + 2)
                    for j in (0, 1):
                        pool.memset(vh[j][:, :, VW:32], 0.0).then_inc(pads, 1)
                    pool.wait_ge(pads, START + 2)
                    for g in (0, 1):
                        pool.tensor_copy(vh[g][:, :, 0:VW], v_all[:, g]).then_inc(v_ready, 1)

                    def side_sum(n):
                        at_step = [0]

                        def after(ins, k=1):
                            ins.then_inc(side_step, 1)
                            at_step[0] += 1
                            wait_apart(pool, "pool", side_step, START + SIDE_STEPS * n + at_step[0])

                        cols = bass.ds(n, 1)
                        pool.dma_start(xr[:], x_rows[bass.ds(n * P, P), :]).then_inc(xr_here, 16)
                        for k in range(TOPK):
                            after(pool.tensor_copy(yidx[k][:], slot_in[:, k, cols]))
                            after(pool.tensor_copy(ygate[k][:], gates[:, k, cols]))
                            pool.indirect_dma_start(out=yg[k][:], out_offset=None, in_=y_dram,
                                                    in_offset=bass.IndirectOffsetOnAxis(ap=yidx[k][:, 0:1], axis=0),
                                                    bounds_check=NB * P - 1, oob_is_err=False).then_inc(y_here, 16)
                        wait_apart(pool, "pool", xr_here, 16 * n + 16)
                        after(pool.tensor_tensor(xr[:], xr[:], bp[:], ALU.add))
                        wait_apart(pool, "pool", y_here, 32 * n + 32)
                        for k in range(TOPK):
                            after(pool.tensor_scalar(yg[k][:], yg[k][:], ygate[k][:, 0:1], None, ALU.mult))
                        after(pool.tensor_tensor(yg[0][:], yg[0][:], xr[:], ALU.add))
                        after(pool.tensor_tensor(side[:, cols, :].rearrange("p b d -> p (b d)"), yg[0][:], yg[1][:], ALU.add))
                        assert at_step[0] == SIDE_STEPS

                    def step(h, j, g, i):
                        side_sum(2 * h)
                        side_sum(2 * h + 1)
                        if g is not None and not isinstance(g, int):
                            pool.wait_ge(pv_done, START + NQ * h + NQ + CREDIT)
                            pool.tensor_copy(vh[j][:, :, 0:VW], v_all[:, bass.ds(h + 2, 1)].rearrange("p h b d -> p (h b) d")).then_inc(v_ready, 1)

                    heads(pool, step)

                @block.vector
                def _(dve):
                    dve.memset(mxp[:], -3.0e38).then_inc(m_chain, 1)
                    dve.wait_ge(m_chain, START + 1)
                    dve.sem_inc(m_done, RING)

                    def tile(g, t):
                        i, c = TILES[t]
                        w = min(CH, (i + 1) * P - c * CH)
                        dve.wait_ge(m_ready, START + NTL * g + t + 1)
                        dve.tensor_reduce(mxp[:, i, c:c + 1], psM[:, t % RING, 0:w], AX, ALU.max).then_inc(m_done, 1)

                    def finish(g):
                        n = [0]

                        def link(ins):
                            n[0] += 1
                            ins.then_inc(m_chain, 1)
                            dve.wait_ge(m_chain, START + M_LINKS * g + n[0] + 1)

                        dve.wait_ge(m_done, START + NTL * g + NTL + RING)
                        link(dve.tensor_reduce(nm[:], mxp[:], AX, ALU.max))
                        link(dve.tensor_scalar(nm[:], nm[:], -1.0, None, ALU.mult))
                        dve.wait_ge(negm_turned, START + g)
                        link(dve.tensor_copy(nm3[:, 0, :], nm[:]))
                        link(dve.tensor_tensor(nr[:], nm[:], nm3[:, 0, :], ALU.subtract))
                        link(dve.tensor_copy(nm3[:, 1, :], nr[:]))
                        link(dve.tensor_tensor(nm3[:, 2, :], nr[:], nm3[:, 1, :], ALU.subtract))
                        assert n[0] == M_LINKS

                    def keep_negm(g):
                        dve.wait_ge(negm_turned, START + g + 1)
                        dve.wait_ge(negm_loaded, START + 16 * SPLIT * g)
                        dve.tensor_copy(mT[:], psMT).then_inc(negm_copied, 1)

                    def normalize(h, qt, q):
                        dve.wait_ge(o_turned, START + q + 1 + CREDIT)
                        o = psN[:, 0:P].rearrange("p (b d) -> p b d", b=4)
                        dve.reciprocal(rden[:], o[:, :, HD:VW]).then_inc(recip, 1)
                        dve.wait_ge(recip, START + q + 1)
                        dve.tensor_tensor(attn[:, 4 * qt:4 * qt + 4, bass.ds(h * HD, HD)], o[:, :, 0:HD],
                                          rden[:].to_broadcast([P, 4, HD]), ALU.mult).then_inc(normed, 1)

                    for t in range(NTL):
                        tile(0, t)
                    finish(0)
                    keep_negm(0)

                    def step(h, j, g, i):
                        for u in range(NQ + 2):
                            if g is not None and u < NQ:
                                for t in tiles_of(u):
                                    tile(g, t)
                                if u == NQ - 4:
                                    finish(g)
                                if u == NQ - 1:
                                    keep_negm(g)
                            if u >= 2 and ends_tile(u - 2):
                                qt = QUADS[u - 2][0]
                                normalize(h, qt, NCH * h + NCH - 1 - qt)

                    heads(dve, step)

                @block.scalar
                def _(act):
                    act.sem_inc(exp_done, RING)

                    def exps(h, u):
                        for m, w in enumerate(widths[u]):
                            n = first_unit[u] + m
                            act.wait_ge(s_ready, START + NU * h + n + 1)
                            if m == 0:
                                act.wait_ge(pv_done, START + NQ * h + u + 1)
                            act.activation(probs[u % 2][:, m, 0:w], psS[:, n % RING, 0:w], ACT.Exp).then_inc(exp_done, 1)

                    def o_copy(h, u):
                        q = NCH * h + NCH - 1 - QUADS[u][0]
                        act.wait_ge(pv_done, START + NQ * h + u + 1 + CREDIT)
                        act.wait_ge(o_turned, START + q + 1)
                        act.copy(oT[(NCH - 1 - QUADS[u][0]) % 2][:], psO[:]).then_inc(o_copied, 1)

                    def step(h, j, g, i):
                        for u in range(NQ):
                            exps(h, u)
                            if u >= 1 and ends_tile(u - 1):
                                o_copy(h, u - 1)
                        o_copy(h, NQ - 1)

                    heads(act, step)

                @block.tensor
                def _(pe):
                    pe.sem_inc(pv_done, CREDIT)
                    pe.sem_inc(o_turned, CREDIT)
                    pe.wait_ge(aug_ones, START + 2)
                    pe.wait_ge(pads, START + 2)

                    def tile(g, jg, t):
                        i, c = TILES[t]
                        w = min(CH, (i + 1) * P - c * CH)
                        diagonal = c == i // 4
                        pe.wait_ge(m_done, START + NTL * g + t + 1)
                        ins = pe.matmul(psM[:, t % RING, 0:w], qa[jg][0:PAIRS * HD, i * P:(i + 1) * P], ka[jg][0:PAIRS * HD, c * CH:c * CH + w],
                                        start=True, stop=not diagonal)
                        if diagonal:
                            ins = pe.matmul(psM[:, t % RING, w - P:w], identb[:], maskS[:], start=False, stop=True)
                        ins.then_inc(m_ready, 1)

                    def scores(h, j, u, g):
                        qt, b = QUADS[u]
                        m, col, w = places(u)[g]
                        n = first_unit[u] + m
                        kb = 4 * b + g
                        if col == 0:
                            pe.wait_ge(exp_done, START + NU * h + before(n) + 1 + RING)
                        out_at = psS[:, n % RING, :]
                        ins = pe.matmul(out_at[:, col:col + w], ka[j][:, kb * P:(kb + 1) * P],
                                        qa[j][:, (qt + 1) * CH - w:(qt + 1) * CH], start=True, stop=b < qt)
                        if b == qt:
                            m = P if w < CH or g == 0 else (g + 1) * P
                            ins = pe.matmul(out_at[:, col:col + m], identb[:], maskT[:, 4 * P - m:4 * P], start=False, stop=True)
                        if col + w == widths[u][places(u)[g][0]]:
                            ins.then_inc(s_ready, 1)

                    def products(h, j, u):
                        qt, b = QUADS[u]
                        pe.wait_ge(exp_done, START + NU * h + first_unit[u + 1] + RING)
                        if b == 0:
                            pe.wait_ge(o_copied, START + NCH * h + NCH - 1 - qt)
                        for g in range(4):
                            m, col, w = places(u)[g]
                            ins = pe.matmul(psO[32 * g:32 * g + 32, CH - w:CH], vh[j][:, 4 * b + g, :],
                                            probs[u % 2][:, m, col:col + w], start=(b == 0), stop=(b == qt),
                                            tile_position=(0, 32 * g))
                        ins.then_inc(pv_done, 1)

                    def turn(h, u, g):
                        qt = QUADS[u][0]
                        q = NCH * h + NCH - 1 - qt
                        pe.wait_ge(o_copied, START + q + 1)
                        pe.wait_ge(normed, START + q)
                        if g is not None:
                            pe.wait_ge(negm_copied, START + g + 1)
                        for b in range(4):
                            ins = pe.matmul(psN[:, 32 * b:32 * b + VW], oT[(NCH - 1 - qt) % 2][:, b * P:(b + 1) * P], con("sel"),
                                            start=True, stop=True)
                        ins.then_inc(o_turned, 1)

                    def turn_negm(g, n):
                        pe.wait_ge(m_chain, START + M_LINKS * g + M_LINKS + 1)
                        pe.wait_ge(normed, START + n)
                        pe.transpose(psMT, nm3[:].rearrange("p c b -> p (c b)"), identb[:]).then_inc(negm_turned, 1)

                    pe.wait_ge(late_loaded[0], START + LATE)
                    pe.wait_ge(early_loaded[0], START + EARLY)
                    for t in range(NTL):
                        tile(0, 0, t)
                    turn_negm(0, 0)

                    def step(h, j, g, i):
                        done = 0
                        for u in range(NQ + 2):
                            tiles = list(tiles_of(u)) if g is not None and u < NQ else []
                            for n in range(4):
                                for t in tiles[n * len(tiles) // 4:(n + 1) * len(tiles) // 4]:
                                    if t == 0:
                                        pe.wait_ge(late_loaded[1 - j], START + LATE * (i + 1 + j))
                                    if t == FIRST_EARLY:
                                        pe.wait_ge(early_loaded[1 - j], START + EARLY * (i + 1 + j))
                                    tile(g, 1 - j, t)
                                if u == 0 and n == 0:
                                    pe.wait_ge(negm_loaded, START + 16 * SPLIT * (h + 1))
                                    pe.wait_ge(v_ready, START + h + 1)
                                if u < NQ:
                                    scores(h, j, u, n)
                            if 1 <= u <= NQ:
                                products(h, j, u - 1)
                            if g is not None and u == NQ - 1:
                                turn_negm(g, NCH * h + done)
                            if u >= 2 and ends_tile(u - 2):
                                turn(h, u - 2, g if u > NQ - 1 else None)
                                done += 1

                    heads(pe, step)

        def stage_output(attn, side):
            scope = ExitStack()
            with scope:
                at_st = [sb(f"at_st{j}", [P, D], scope=scope) for j in range(2)]
                aT = [sb(f"aT{j}", [P, KD, P], scope=scope) for j in range(2)]
                res = [sb(f"res{j}", [P, D], scope=scope) for j in range(2)]
                psA = [scope.enter_context(nc.psum_tensor(f"psA{j}", [P, CH], F32)) for j in range(2)]
                psP = [scope.enter_context(nc.psum_tensor(f"psP{j}", [P, CH], F32)) for j in range(2)]
                staged = sems("staged")
                a_turned, aT_ready, projected = sems("a_turned"), sems("aT_ready"), sems("projected")
                res_ready, res_stored = sems("res_ready"), sems("res_stored")
                block = scope.enter_context(nc.Block())
                NI = NT // 2

                @block.sync
                def _(sp):
                    with sp.Fori(0, NI) as i:
                        for j in (0, 1):
                            sp.wait_ge(res_ready[j], START + i + 1)
                            sp.dma_start(out_rows[bass.ds((2 * i + j) * P, P), :], res[j][:]).then_inc(res_stored[j], 16)
                    for j in (0, 1):
                        sp.wait_ge(res_stored[j], START + 16 * NI)

                @block.gpsimd
                def _(pool):
                    start_counts(pool)
                    with pool.Fori(0, NI) as i:
                        for j in (0, 1):
                            pool.wait_ge(a_turned[j], START + i)
                            pool.tensor_copy(at_st[j][:], attn[:, bass.ds(2 * i + j, 1), :].rearrange("p b d -> p (b d)")).then_inc(staged[j], 1)

                @block.scalar
                def _(act):
                    with act.Fori(0, NI) as i:
                        for j in (0, 1):
                            act.wait_ge(a_turned[j], START + i + 1)
                            act.wait_ge(projected[j], START + i)
                            act.copy(aT[j][:], psA[j][:, 0:D].rearrange("p (k t) -> p k t", k=KD)).then_inc(aT_ready[j], 1)

                @block.vector
                def _(dve):
                    with dve.Fori(0, NI) as i:
                        for j in (0, 1):
                            dve.wait_ge(projected[j], START + i + 1)
                            dve.wait_ge(res_stored[j], START + 16 * i)
                            dve.tensor_tensor(res[j][:], psP[j][:, 0:D], side[:, bass.ds(2 * i + j, 1), :].rearrange("p b d -> p (b d)"),
                                              ALU.add).then_inc(res_ready[j], 1)

                @block.tensor
                def _(pe):
                    def turn(i, j):
                        pe.wait_ge(staged[j], START + i + 1)
                        pe.wait_ge(aT_ready[j], START + i)
                        for k in range(KD):
                            ins = pe.transpose(psA[j][:, k * P:(k + 1) * P], at_st[j][:, k * P:(k + 1) * P], ident)
                        ins.then_inc(a_turned[j], 1)

                    def project(i, j):
                        pe.wait_ge(aT_ready[j], START + i + 1)
                        pe.wait_ge(res_ready[j], START + i)
                        for k in range(KD):
                            ins = pe.matmul(psP[j][:, 0:D], aT[j][:, k, :], wp[:, k, :], start=(k == 0), stop=(k == KD - 1))
                        ins.then_inc(projected[j], 1)

                    turn(0, 0)
                    with pe.Fori(0, NI - 1) as i:
                        turn(i, 1)
                        project(i, 0)
                        turn(i + 1, 0)
                        project(i, 1)
                    turn(NI - 1, 1)
                    project(NI - 1, 0)
                    project(NI - 1, 1)

        stage_tokens()
        stage_queries()
        stage_experts()
        weights.close()
        attn, side = sb("attn", [P, NT, D]), sb("side", [P, NT, D])
        stage_attend(attn, side)
        stage_output(attn, side)


def kernel(L0_attn_hidden_states, L0_attn_c_attn_w, L0_attn_c_attn_b, L0_attn_c_proj_w, L0_attn_c_proj_b,
           L0_ffn_router_w, L0_ffn_w1, L0_ffn_w2):
    import concourse.bacc as bacc
    from concourse.bass_utils import run_bass_kernel_spmd

    nc = bacc.Bacc("TRN2", target_bir_lowering=False, num_devices=1)
    arrays = {
        "x": L0_attn_hidden_states, "w_attn": L0_attn_c_attn_w, "b_attn": np.asarray(L0_attn_c_attn_b)[None, :],
        "b_qk": np.asarray(L0_attn_c_attn_b)[:2 * D].reshape(4, P).T, "w_proj": L0_attn_c_proj_w, "b_proj": np.asarray(L0_attn_c_proj_b)[None, :],
        "w_router": np.asarray(L0_ffn_router_w).T, "w1": L0_ffn_w1, "w2": L0_ffn_w2, "consts": const_array(),
    }
    arrays = {n: np.ascontiguousarray(a) for n, a in arrays.items()}
    args = [nc.dram_tensor(n, a.shape, mybir.dt.from_np(a.dtype), kind="ExternalInput").ap() for n, a in arrays.items()]
    out = nc.dram_tensor("out", (1, S, D), F32, kind="ExternalOutput").ap()
    build(nc, *args, out)
    r = run_bass_kernel_spmd(nc, [arrays], core_ids=[0])
    return r.results[0]["out"]
```

```python
import numpy as np

import concourse.bass as bass
from concourse import mybir

P = 128
F32 = mybir.dt.float32
BF16 = mybir.dt.bfloat16
I32 = mybir.dt.int32
ALU = mybir.AluOpType
ACT = mybir.ActivationFunctionType
AX = mybir.AxisListType.X

S, D, H, HD = 4096, 256, 16, 16
E, F, CAP = 8, 1024, 1280
TOPK = 2
NT = S // P
CH = 512
NCH = S // CH
KD = D // P
KF = F // P
VW = HD + 1
NB = 71
JG = 20
NEG = -1.0e37
FAR = float(1 << 20)
EPS = 1e-5
SPLIT = 3
PAIRS = 6
AUG = PAIRS * HD + SPLIT
QUADS = [(qt, b) for qt in range(NCH - 1, -1, -1) for b in range(qt + 1)]
WHOLE = [(kb, kb, 0, CH) for kb in range(4)]
EVEN = (4 + 3 + 2 + 1) * P // 4
DIAGONAL = [(0, 0, CH - EVEN, CH), (1, 1, CH - EVEN, CH), (2, 2, 2 * P, CH), (3, 3, 3 * P, CH),
            (1, 2, P, CH - EVEN), (0, 3, 0, CH - EVEN)]
NQ = len(QUADS)
HALF = NT // 2
TILES_LATE = [(i, c) for c in range(NCH - 1, -1, -1) for i in range(max(4 * c, HALF), NT)]
TILES_EARLY = [(i, c) for c in range(NCH // 2 - 1, -1, -1) for i in range(4 * c, HALF)]
NTL = len(TILES_LATE) + len(TILES_EARLY)
LATE_OVER = NQ - 6
START = 1
CREDIT = 2
RING = 3


def tile_width(tile):
    i, c = tile
    return min(CH, (i + 1) * P - c * CH)


def ends_tile(u):
    return u % NQ == NQ - 1 or QUADS[u % NQ + 1][0] != QUADS[u % NQ][0]


def spread():
    COST, NORMALIZE, FINISH = 64, 700, 1200
    for ahead in range(len(TILES_EARLY)):
        stream = TILES_EARLY[ahead:] + TILES_LATE + TILES_EARLY[:ahead]
        early_end, late_end = len(TILES_EARLY) - ahead, NTL - ahead
        total = sum(tile_width(t) + COST for t in stream) + NCH * NORMALIZE + 2 * FINISH
        beside, t, spent = [], 0, 0
        for u in range(NQ):
            spent += NORMALIZE if ends_tile(u - 3) else 0
            first = t
            while t < NTL and (spent < total * (u + 1) / NQ or u == NQ - 1):
                spent += tile_width(stream[t]) + COST
                t += 1
                if t in (early_end, late_end):
                    spent += FINISH
            beside.append(range(first, t))
        early_over = next(u for u in range(NQ) if early_end - 1 in beside[u])
        late_over = next(u for u in range(NQ) if late_end - 1 in beside[u])
        if late_over <= LATE_OVER:
            return ahead, beside, early_over, late_over


AHEAD, BESIDE, EARLY_OVER, LATE_OVER = spread()
STREAM = TILES_EARLY[AHEAD:] + TILES_LATE + TILES_EARLY[:AHEAD]
LATE_AT, AHEAD_AT = len(TILES_EARLY) - AHEAD, NTL - AHEAD
FIRST_TILES = TILES_LATE + TILES_EARLY[:AHEAD]


def const_layout():
    at, cols = {}, 0
    for name, width in (("ident", P), ("tri", P), ("mult", 3 * NT), ("eid", E), ("grid", JG),
                        ("block", NB), ("tok", NT), ("scan", TOPK * E * NT), ("maskT", 4 * P), ("maskS", P)):
        at[name] = (cols, width)
        cols += width
    return at, cols


def const_array():
    at, cols = const_layout()
    c = np.zeros((P, cols), np.float32)

    def put(name, value):
        a, w = at[name]
        c[:, a:a + w] = np.broadcast_to(value, (P, w))

    r = np.arange(P)
    put("ident", np.eye(P))
    put("tri", r[:, None] < r[None, :])
    first, second = S // 3, 2 * S // 3
    pos = r[:, None] + P * np.arange(NT)[None, :]
    regions = [pos < first, (pos >= first) & (pos < second), pos >= second]
    put("mult", np.concatenate([np.float32(1.0) + np.float32(0.6) * g.astype(np.float32) for g in regions], 1))
    put("eid", np.arange(E) - E)
    put("grid", P * np.arange(JG))
    put("block", np.arange(NB))
    put("tok", pos)
    put("scan", (np.arange(TOPK * E * NT) % NT != 0))
    put("maskT", np.where(r[:, None] > np.arange(-3 * P, P)[None, :], NEG, 0.0))
    put("maskS", np.where(r[None, :] > r[:, None], NEG, 0.0))
    return c


def build(nc, x, w_attn, b_attn, b_qk, w_proj, b_proj, w_router, w1, w2, consts, out):
    at, CW = const_layout()
    from contextlib import ExitStack
    ctx = ExitStack()
    with ctx:
        def sb(name, shape, dt=F32, scope=ctx):
            return scope.enter_context(nc.sbuf_tensor(name, shape, dt))

        fresh = []

        def sem(name):
            fresh.append(ctx.enter_context(nc.semaphore(name)))
            return fresh[-1]

        def start_counts(pool):
            for s in fresh:
                pool.sem_inc(s, START)
            fresh.clear()

        def pool_dma_sems(name, n=2):
            return [ctx.enter_context(nc.semaphore(f"{name}{j}")) for j in range(n)]

        def sems(name, n=2):
            return [sem(f"{name}{j}") for j in range(n)]

        x_rows = x.rearrange("a s d -> (a s) d")
        out_rows = out.rearrange("a s d -> (a s) d")
        xn_dram = nc.dram_tensor("xn_scratch", [S, D], F32, kind="Internal").ap()
        qk_dram = nc.dram_tensor("qk_scratch", [2, SPLIT, D, S], BF16, kind="Internal").ap()
        list_dram = nc.dram_tensor("list_scratch", [NB * P, 1], F32, kind="Internal").ap()
        y_dram = nc.dram_tensor("y_scratch", [NB * P, D], F32, kind="Internal").ap()

        cst = sb("cst", [P, CW])

        def con(name):
            a, w = at[name]
            return cst[:, a:a + w]

        ident = con("ident")
        identb = sb("identb", [P, P], BF16)
        maskT = sb("maskT", [P, 4 * P], BF16)
        maskS = sb("maskS", [P, P], BF16)
        ones = sb("ones", [P, P])
        eps = sb("eps", [P, 1])
        wqk = sb("wqk", [P, KD, 2 * D])
        wv = sb("wv", [P, KD, D + E])
        bv = sb("bv", [P, D])
        bqk = sb("bqk", [P, 4])
        bqk4 = sb("bqk4", [P, 4])
        wp = sb("wp", [P, KD, D])
        bp = sb("bp", [P, D])
        v_all = sb("v_all", [P, H, NT, VW])
        logits = sb("logits", [P, NT, E])
        gates = sb("gates", [P, TOPK, NT])
        slot_out = sb("slot_out", [P, TOPK, NT], I32)
        slot_in = sb("slot_in", [P, TOPK, NT], I32)
        expert_of = sb("expert_of", [P, NB], I32)

        passed = {name: sem(f"passed_{name}") for name in ("sp", "pool", "dve")}

        def wait_apart(eng, name, semaphore, value):
            eng.wait_ge(semaphore, value)
            eng.sem_inc(passed[name], 1)

        s_const = sem("s_const")
        s_vec0 = sem("s_vec0")
        s_pool0 = sem("s_pool0")

        weights = ctx.enter_context(ExitStack())
        w1_sb = sb("w1_sb", [P, KD, E, F], scope=weights)
        w2_sb = sb("w2_sb", [P, E, KF, D], scope=weights)
        lent = w2_sb[:].rearrange("p e k d -> p (e k d)")
        xT_all = lent[:, E * F // 2 * KD:].rearrange("p (c x) -> p c x", c=NCH)
        half = 4 * D
        x_st = [lent[:, j * half:(j + 1) * half].rearrange("p (b d) -> p b d", b=4) for j in (0, 1)]
        xn_st = [lent[:, j * half:(j + 1) * half].rearrange("p (b d) -> p b d", b=4) for j in (2, 3)]
        xT_st = [lent[:, j * half:(j + 1) * half].rearrange("p (k s) -> p k s", k=KD) for j in (4, 5)]
        w1_dram = w1.rearrange("e (k p) f -> e p k f", p=P)
        w2_dram = w2.rearrange("e (k p) d -> e p k d", p=P)

        w1_loaded = sem("w1_loaded")
        w2_loaded = sem("w2_loaded")

        def stage_tokens():
            scope = ExitStack()
            with scope:
                stats = [sb(f"stats{j}", [P, 4, 6], scope=scope) for j in range(2)]
                mv = [sb(f"mv{j}", [P, 4, 2], scope=scope) for j in range(2)]
                std = [sb(f"std{j}", [P, 4], scope=scope) for j in range(2)]
                rstd = [sb(f"rstd{j}", [P, 4], scope=scope) for j in range(2)]
                psT = [scope.enter_context(nc.psum_tensor(f"psT{j}", [P, KD, CH], F32)) for j in range(2)]
                psV = scope.enter_context(nc.psum_tensor("psV", [P, 4, CH], F32))
                x_loaded = sems("x_loaded")
                st_ready, mv_ready, std_ready = sem("st_ready"), sems("mv_ready"), sems("std_ready")
                rstd_ready = sem("rstd_ready")
                xn_ready, xn_stored = sems("xn_ready"), sems("xn_stored")
                xT_in_psum, xT_ready, xT_kept = sems("xT_in_psum"), sems("xT_ready"), sems("xT_kept")
                v_in_psum, v_out = sem("v_in_psum"), sem("v_out")
                x_blocks = x_rows.rearrange("(c b p) d -> c p b d", p=P, b=4)
                xn_blocks = xn_dram.rearrange("(c b p) d -> c p b d", p=P, b=4)
                block = scope.enter_context(nc.Block())

                @block.sync
                def _(sp):
                    sp.dma_start(x_st[0], x_blocks[0]).then_inc(x_loaded[0], 16)
                    sp.dma_start(cst[:], consts).then_inc(s_const, 16)
                    sp.dma_start(wv[:, :, 0:D], w_attn[:, 2 * D:3 * D].rearrange("(k p) n -> p k n", p=P)).then_inc(s_const, 16)
                    sp.dma_start(wv[:, :, D:D + E], w_router.rearrange("(k p) e -> p k e", p=P)).then_inc(s_const, 16)
                    sp.dma_start(bv[:], b_attn[:, 2 * D:3 * D].to_broadcast([P, D])).then_inc(s_const, 16)
                    sp.dma_start(x_st[1], x_blocks[1]).then_inc(x_loaded[1], 16)
                    for e in (0, 1):
                        sp.dma_start(w1_sb[:, :, e, :], w1_dram[e]).then_inc(w1_loaded, 16)
                    with sp.Fori(1, NCH // 2) as i:
                        for j in (0, 1):
                            sp.wait_ge(xn_ready[j], START + 4 * i)
                            sp.dma_start(x_st[j], x_blocks[bass.ds(2 * i + j, 1)].rearrange("c p b d -> (c p) b d")).then_inc(x_loaded[j], 16)
                            sp.dma_start(w1_sb[:, :, bass.ds(2 * i + j, 1), :].rearrange("p k e f -> p (k e) f"),
                                         w1_dram[bass.ds(2 * i + j, 1)].rearrange("e p k f -> (e p) k f")).then_inc(w1_loaded, 16)
                    sp.dma_start(wqk[:], w_attn[:, 0:2 * D].rearrange("(k p) n -> p k n", p=P)).then_inc(s_const, 16)
                    sp.dma_start(bqk[:], b_qk).then_inc(s_const, 16)
                    sp.dma_start(wp[:], w_proj.rearrange("(k p) n -> p k n", p=P)).then_inc(s_const, 16)
                    sp.dma_start(bp[:], b_proj.to_broadcast([P, D])).then_inc(s_const, 16)

                @block.gpsimd
                def _(pool):
                    start_counts(pool)
                    pool.memset(ones[:], 1.0).then_inc(s_pool0, 1)
                    pool.memset(eps[:], EPS).then_inc(s_pool0, 1)
                    pool.memset(v_all[:, :, :, HD:VW], 1.0).then_inc(s_pool0, 1)
                    with pool.Fori(0, NCH // 2) as i:
                        for j in (0, 1):
                            pool.wait_ge(xT_ready[j], START + 2 * i + 2)
                            pool.tensor_copy(xT_all[:, bass.ds(2 * i + j, 1), :].rearrange("p c x -> p (c x)"),
                                             xT_st[j].rearrange("p k s -> p (k s)")).then_inc(xT_kept[j], 1)

                def chunks(eng, first, both, last):
                    first()
                    with eng.Fori(0, NCH // 2 - 1) as i:
                        both(2 * i, i, 0)
                        both(2 * i + 1, i, 1)
                    both(NCH - 2, NCH // 2 - 1, 0)
                    last(NCH - 1, NCH // 2 - 1, 1)

                @block.vector
                def _(dve):
                    def normalize(n, i, j):
                        dve.wait_ge(x_loaded[j], START + 16 * i + 16)
                        for b in range(4):
                            dve.bn_stats(stats[j][:, b, :], x_st[j][:, b, :]).then_inc(st_ready, 1)
                        wait_apart(dve, "dve", st_ready, START + 4 * n + 4)
                        for b in range(4):
                            dve.bn_aggr(mv[j][:, b, :], stats[j][:, b, :]).then_inc(mv_ready[j], 1)
                        dve.wait_ge(std_ready[j], START + i + 1)
                        dve.reciprocal(rstd[j][:], std[j][:]).then_inc(rstd_ready, 1)
                        dve.wait_ge(rstd_ready, START + n + 1)
                        dve.wait_ge(xT_in_psum[j], START + i)
                        dve.wait_ge(xn_stored[j], START + 16 * i)
                        for b in range(4):
                            dve.tensor_scalar(xn_st[j][:, b, :], x_st[j][:, b, :], mv[j][:, b, 0:1],
                                              rstd[j][:, b:b + 1], ALU.subtract, ALU.mult).then_inc(xn_ready[j], 1)

                    def keep_turned(n, i, j):
                        dve.wait_ge(xT_in_psum[j], START + i + 1)
                        dve.wait_ge(xT_kept[j], START + i)
                        dve.wait_ge(v_in_psum, START + 2 * i)
                        dve.tensor_copy(xT_st[j][:, 1, :], psT[j][:, 1, :]).then_inc(xT_ready[j], 1)

                    def keep_values(n, i, j):
                        dve.wait_ge(v_in_psum, START + n + 1)
                        for b in range(4):
                            dve.tensor_tensor(v_all[:, :, bass.ds(4 * n + b, 1), 0:HD].rearrange("p h b d -> p h (b d)"),
                                              psV[:, b, 0:D].rearrange("p (h d) -> p h d", h=H),
                                              bv[:].rearrange("p (h d) -> p h d", h=H), ALU.add)
                        dve.tensor_copy(logits[:, bass.ds(4 * n, 4), :], psV[:, :, D:D + E]).then_inc(v_out, 1)

                    def both(n, i, j):
                        keep_turned(n, i, j)
                        normalize(n + 1, i + j, 1 - j)
                        keep_values(n, i, j)

                    def last(n, i, j):
                        keep_turned(n, i, j)
                        keep_values(n, i, j)

                    def begin():
                        normalize(0, 0, 0)
                        dve.wait_ge(s_const, START + 64)
                        dve.tensor_copy(identb[:], ident).then_inc(s_vec0, 1)
                        dve.tensor_copy(maskT[:], con("maskT")).then_inc(s_vec0, 1)
                        dve.tensor_copy(maskS[:], con("maskS")).then_inc(s_vec0, 1)

                    chunks(dve, begin, both, last)

                @block.scalar
                def _(act):
                    act.wait_ge(s_pool0, START + 3)

                    def normalize(n, i, j):
                        act.wait_ge(mv_ready[j], START + 4 * i + 4)
                        act.wait_ge(rstd_ready, START + 2 * i)
                        act.activation(std[j][:], mv[j][:, :, 1], ACT.Sqrt, bias=eps[:, 0:1], scale=1.0).then_inc(std_ready[j], 1)
                        act.wait_ge(xn_ready[j], START + 4 * i + 4)
                        act.dma_start(xn_blocks[bass.ds(n, 1)].rearrange("c p b d -> (c p) b d"), xn_st[j]).then_inc(xn_stored[j], 16)

                    def keep_turned(n, i, j):
                        act.wait_ge(xT_in_psum[j], START + i + 1)
                        act.wait_ge(xT_kept[j], START + i)
                        act.wait_ge(v_in_psum, START + 2 * i)
                        act.copy(xT_st[j][:, 0, :], psT[j][:, 0, :]).then_inc(xT_ready[j], 1)

                    def both(n, i, j):
                        keep_turned(n, i, j)
                        normalize(n + 1, i + j, 1 - j)

                    chunks(act, lambda: normalize(0, 0, 0), both, keep_turned)
                    for j in (0, 1):
                        act.wait_ge(xn_stored[j], START + 16 * (NCH // 2))

                @block.tensor
                def _(pe):
                    pe.wait_ge(s_const, START + 64)

                    def turn(n, i, j):
                        pe.wait_ge(xn_ready[j], START + 4 * i + 4)
                        pe.wait_ge(xT_ready[j], START + 2 * i)
                        for k in range(KD):
                            for b in range(4):
                                ins = pe.transpose(psT[j][:, k, b * P:(b + 1) * P], xn_st[j][:, b, k * P:(k + 1) * P], ident)
                        ins.then_inc(xT_in_psum[j], 1)

                    def values(n, i, j):
                        pe.wait_ge(xT_ready[j], START + 2 * i + 2)
                        pe.wait_ge(v_out, START + n)
                        for b in range(4):
                            for k in range(KD):
                                ins = pe.matmul(psV[:, b, 0:D + E], xT_st[j][:, k, b * P:(b + 1) * P], wv[:, k, :],
                                                start=(k == 0), stop=(k == KD - 1))
                        ins.then_inc(v_in_psum, 1)

                    def both(n, i, j):
                        values(n, i, j)
                        turn(n + 1, i + j, 1 - j)

                    chunks(pe, lambda: turn(0, 0, 0), both, values)

        def stage_queries():
            scope = ExitStack()
            with scope:
                t_st = [sb(f"t_st{q}", [P, CH], scope=scope) for q in range(2)]
                r_both = sb("r_both", [P, 2 * CH], scope=scope)
                r_st = [r_both[:, q * CH:(q + 1) * CH] for q in range(2)]
                big = TOPK * NT * E
                onehot = sb("onehot", [P, TOPK, NT, E], scope=scope)
                work = sb("work", [P, 3, big], scope=scope)
                tmp = work[:, 0].rearrange("p (k b e) -> p k b e", k=TOPK, b=NT)
                cnt = work[:, 1].rearrange("p (k e b) -> p k e b", k=TOPK, e=E)
                inc = work[:, 2].rearrange("p (k e b) -> p k e b", k=TOPK, e=E)
                late_parts = work[:].bitcast(BF16).rearrange("p a x -> p (a x)").rearrange("p (u c s) -> p u c s", u=2, c=SPLIT)
                assert 3 * big * 2 == 2 * SPLIT * CH
                s_st = [sb(f"s_st{u}", [P, SPLIT, CH], BF16, scope=scope)[:] for u in range(2)] + [late_parts[:, u] for u in range(2)]
                m1 = sb("m1", [P, NT], scope=scope)
                m2 = sb("m2", [P, NT], scope=scope)
                fst = sb("fst", [P, NT], scope=scope)
                e2 = sb("e2", [P, NT], scope=scope)
                pos = sb("pos", [P, TOPK, NT], scope=scope)
                keep = sb("keep", [P, TOPK, NT], scope=scope)
                tot = sb("tot", [P, TOPK, E], scope=scope)
                nsum = sb("nsum", [P, E], scope=scope)
                nblk = sb("nblk", [P, E], scope=scope)
                endb = sb("endb", [P, E], scope=scope)
                base = sb("base", [P, TOPK, E], scope=scope)
                blk = r_both[:, 0:NB * E].rearrange("p (b e) -> p b e", e=E)
                eidf = sb("eidf", [P, NB], scope=scope)
                zero = sb("zero", [NB, P], scope=scope)
                GROUP = 4
                sidx = [sb(f"sidx{j}", [P, TOPK, GROUP], I32, scope=scope) for j in range(2)]
                stok = [sb(f"stok{j}", [P, GROUP], scope=scope) for j in range(2)]
                psQ = [scope.enter_context(nc.psum_tensor(f"psQ{q}", [P, CH], F32)) for q in range(2)]
                psR = [scope.enter_context(nc.psum_tensor(f"psR{q}", [P, TOPK, NT, E], F32)) for q in range(2)]
                q_in_psum, t_ready, s1_ready = sems("q_in_psum"), sems("t_ready"), sems("s1_ready")
                r_ready, s2_ready, s3_ready, q_stored = sems("r_ready"), sems("s2_ready"), sems("s3_ready"), sems("q_stored", 4)
                counted, gap_ready, e2_ready = sem("counted"), sem("gap_ready"), sem("e2_ready")
                ONEHOT_LINKS = 11
                slots_ready, zero_ready, listed = sem("slots_ready"), sem("zero_ready"), pool_dma_sems("listed")
                idx_ready, route, routed = sem("idx_ready"), sem("route"), sem("routed")
                list_zeroed = sem("list_zeroed")
                units = [(fc, fc % 2, fc // 2) for fc in range(4)]
                block = scope.enter_context(nc.Block())

                @block.sync
                def _(sp):
                    for e in range(E // 2):
                        sp.dma_start(w2_sb[:, e], w2_dram[e]).then_inc(w2_loaded, 16)
                    sp.wait_ge(zero_ready, START + 1)
                    sp.dma_start(list_dram.rearrange("(b p) o -> b (p o)", p=P), zero[:]).then_inc(list_zeroed, 16)
                    with sp.Fori(0, NCH // 2) as m:
                        for i in (2 * m, 2 * m + 1):
                            for fc, q, r in units:
                                sp.wait_ge(s3_ready[q], START + 2 * i + r + 1)
                                dst = qk_dram[fc // 2, :, (fc % 2) * P:(fc % 2 + 1) * P, bass.ds(i * CH, CH)]
                                sp.dma_start(dst.rearrange("c p s -> p c s"), s_st[fc]).then_inc(q_stored[fc], 16)
                        sp.dma_start(w2_sb[:, bass.ds(E // 2 + m, 1)].rearrange("p e k d -> p (e k) d"),
                                     w2_dram[bass.ds(E // 2 + m, 1)].rearrange("e p k d -> (e p) k d")).then_inc(w2_loaded, 16)
                    for fc in range(4):
                        sp.wait_ge(q_stored[fc], START + 16 * NCH)

                @block.gpsimd
                def _(pool):
                    start_counts(pool)
                    pool.memset(zero[:], 0.0).then_inc(zero_ready, 1)
                    pool.wait_ge(list_zeroed, START + 16)
                    pool.wait_ge(slots_ready, START + 2)

                    def scatter(i, j, first=False):
                        g = 2 * i + j
                        if not first:
                            pool.wait_ge(listed[j], 16 * TOPK * GROUP * i)
                        pool.tensor_copy(sidx[j][:], slot_out[:, :, bass.ds(GROUP * g, GROUP)]).then_inc(idx_ready, 1)
                        pool.tensor_copy(stok[j][:], con("tok")[:, bass.ds(GROUP * g, GROUP)]).then_inc(idx_ready, 1)
                        wait_apart(pool, "pool", idx_ready, START + 2 * g + 2)
                        for k in range(TOPK):
                            for b in range(GROUP):
                                pool.indirect_dma_start(out=list_dram, out_offset=bass.IndirectOffsetOnAxis(ap=sidx[j][:, k, b:b + 1], axis=0),
                                                        in_=stok[j][:, b:b + 1], in_offset=None, bounds_check=NB * P - 1,
                                                        oob_is_err=False).then_inc(listed[j], 16)

                    scatter(0, 0, first=True)
                    scatter(0, 1, first=True)
                    with pool.Fori(1, NT // GROUP // 2) as i:
                        scatter(i, 0)
                        scatter(i, 1)
                    for j in (0, 1):
                        pool.wait_ge(listed[j], 16 * TOPK * NT // 2)

                @block.scalar
                def _(act):
                    act.wait_ge(s_const, START + 128)
                    act.mul(bqk4[:, 0:2], bqk[:, 0:2], 0.25)
                    act.copy(bqk4[:, 2:4], bqk[:, 2:4]).then_inc(s_vec0, 1)
                    act.wait_ge(s_vec0, START + 4)
                    act.wait_ge(gap_ready, START + 1)
                    act.activation(e2[:], e2[:], ACT.Exp).then_inc(e2_ready, 1)
                    act.wait_ge(routed, START + 1)
                    with act.Fori(0, NCH) as i:
                        for fc, q, r in units:
                            act.wait_ge(q_in_psum[q], START + 2 * i + r + 1)
                            act.wait_ge(r_ready[q], START + 2 * i + r)
                            act.activation(t_st[q][:], psQ[q][:], ACT.Identity, bias=bqk4[:, fc:fc + 1],
                                           scale=0.25 if fc < 2 else 1.0).then_inc(t_ready[q], 1)
                            act.wait_ge(t_ready[q], START + 2 * i + r + 1)
                            act.wait_ge(q_stored[fc], START + 16 * i)
                            act.copy(s_st[fc][:, 0, :], t_st[q][:]).then_inc(s1_ready[q], 1)

                @block.vector
                def _(dve):
                    n = [0]

                    def link(ins):
                        n[0] += 1
                        ins.then_inc(route, 1)
                        dve.wait_ge(route, START + n[0])

                    def wide(a, shape):
                        return a.to_broadcast(shape)

                    eid = con("eid")
                    SH = [P, NT, E]
                    lg = logits[:]
                    for k, m in ((0, m1), (1, m2)):
                        link(dve.tensor_reduce(m[:], lg, AX, ALU.max))
                        link(dve.tensor_tensor(tmp[:, 0], lg, wide(m[:].unsqueeze(2), SH), ALU.is_equal))
                        link(dve.tensor_tensor(tmp[:, 0], tmp[:, 0], wide(eid.unsqueeze(1), SH), ALU.mult))
                        link(dve.tensor_reduce(fst[:], tmp[:, 0], AX, ALU.min))
                        link(dve.tensor_tensor(onehot[:, k], wide(eid.unsqueeze(1), SH), wide(fst[:].unsqueeze(2), SH), ALU.is_equal))
                        if k == 0:
                            link(dve.scalar_tensor_tensor(out=tmp[:, 1], in0=onehot[:, 0], scalar=-3.0e38, in1=lg,
                                                          op0=ALU.mult, op1=ALU.add))
                            lg = tmp[:, 1]
                    dve.tensor_tensor(e2[:], m2[:], m1[:], ALU.subtract).then_inc(gap_ready, 1)
                    assert n[0] == ONEHOT_LINKS
                    dve.wait_ge(e2_ready, START + 1)
                    link(dve.tensor_scalar(m1[:], e2[:], 1.0, None, ALU.add))
                    link(dve.reciprocal(gates[:, 0], m1[:]))
                    link(dve.tensor_tensor(gates[:, 1], e2[:], gates[:, 0], ALU.mult))
                    dve.wait_ge(counted, START + 2)
                    link(dve.tensor_copy(cnt.rearrange("p k e b -> p k b e"), psR[1][:]))
                    f = "p k e b -> p (k e b)"
                    link(dve.tensor_tensor_scan(inc.rearrange(f), con("scan"), cnt.rearrange(f), 0.0, ALU.mult, ALU.add))
                    link(dve.tensor_scalar(tot[:], inc[:, :, :, NT - 1], float(CAP), None, ALU.min))
                    link(dve.tensor_tensor(inc, inc, cnt, ALU.subtract))
                    for k in range(TOPK):
                        link(dve.tensor_tensor(tmp[:, k], inc[:, k].rearrange("p e b -> p b e"), psR[0][:, k], ALU.add))
                        link(dve.tensor_tensor(tmp[:, k], tmp[:, k], onehot[:, k], ALU.mult))
                        link(dve.tensor_reduce(pos[:, k], tmp[:, k], AX, ALU.add))
                    link(dve.tensor_tensor(nsum[:], tot[:, 0], tot[:, 1], ALU.add))
                    link(dve.tensor_tensor(tmp.rearrange("p k b e -> p (k b e)")[:, 0:E * JG].rearrange("p (e j) -> p e j", e=E),
                                           wide(nsum[:].unsqueeze(2), [P, E, JG]), wide(con("grid").unsqueeze(1), [P, E, JG]), ALU.is_gt))
                    link(dve.tensor_reduce(nblk[:], tmp.rearrange("p k b e -> p (k b e)")[:, 0:E * JG].rearrange("p (e j) -> p e j", e=E),
                                           AX, ALU.add))
                    link(dve.tensor_tensor_scan(endb[:], ones[:, 0:E], nblk[:], 0.0, ALU.mult, ALU.add))
                    link(dve.tensor_tensor(base[:, 0], endb[:], nblk[:], ALU.subtract))
                    link(dve.tensor_scalar(base[:, 0], base[:, 0], float(P), None, ALU.mult))
                    link(dve.tensor_tensor(base[:, 1], base[:, 0], tot[:, 0], ALU.add))
                    link(dve.tensor_scalar(keep[:], pos[:], float(CAP), None, ALU.is_lt))
                    for k in range(TOPK):
                        link(dve.tensor_tensor(tmp[:, k], onehot[:, k], wide(base[:, k].unsqueeze(1), SH), ALU.mult))
                        link(dve.tensor_reduce(m1[:], tmp[:, k], AX, ALU.add))
                        link(dve.tensor_tensor(pos[:, k], pos[:, k], m1[:], ALU.add))
                    link(dve.tensor_tensor(gates[:], gates[:], keep[:], ALU.mult))
                    link(dve.tensor_tensor(pos[:], pos[:], keep[:], ALU.mult))
                    dve.tensor_copy(slot_in[:], pos[:]).then_inc(slots_ready, 1)
                    link(dve.tensor_scalar(keep[:], keep[:], -FAR, FAR, ALU.mult, ALU.add))
                    link(dve.tensor_tensor(pos[:], pos[:], keep[:], ALU.add))
                    dve.tensor_copy(slot_out[:], pos[:]).then_inc(slots_ready, 1)
                    link(dve.tensor_tensor(blk, wide(endb[:].unsqueeze(1), [P, NB, E]), wide(con("block").unsqueeze(2), [P, NB, E]), ALU.is_le))
                    link(dve.tensor_reduce(eidf[:], blk, AX, ALU.add))
                    link(dve.tensor_scalar(eidf[:], eidf[:], float(E - 1), None, ALU.min))
                    dve.tensor_copy(expert_of[:], eidf[:]).then_inc(routed, 1)
                    dve.wait_ge(s_pool0, START + 3)
                    for h in range(3):
                        dve.tensor_tensor(v_all[:, h], v_all[:, h],
                                          wide(con("mult")[:, h * NT:(h + 1) * NT].unsqueeze(2), [P, NT, VW]), ALU.mult)
                    with dve.Fori(0, NCH) as i:
                        for fc, q, r in units:
                            dve.wait_ge(s1_ready[q], START + 2 * i + r + 1)
                            dve.tensor_tensor(r_st[q], t_st[q][:], s_st[fc][:, 0, :], ALU.subtract).then_inc(r_ready[q], 1)
                            dve.wait_ge(r_ready[q], START + 2 * i + r + 1)
                            dve.tensor_copy(s_st[fc][:, 1, :], r_st[q]).then_inc(s2_ready[q], 1)
                            dve.wait_ge(s2_ready[q], START + 2 * i + r + 1)
                            dve.tensor_tensor(s_st[fc][:, 2, :], r_st[q], s_st[fc][:, 1, :], ALU.subtract).then_inc(s3_ready[q], 1)

                @block.tensor
                def _(pe):
                    pe.wait_ge(s_const, START + 128)

                    def count():
                        pe.wait_ge(route, START + ONEHOT_LINKS)
                        rows = onehot[:].rearrange("p k b e -> p (k b e)")
                        pe.matmul(psR[0][:].rearrange("p k b e -> p (k b e)"), con("tri"), rows, start=True, stop=True).then_inc(counted, 1)
                        pe.matmul(psR[1][:].rearrange("p k b e -> p (k b e)"), ones[:], rows, start=True, stop=True).then_inc(counted, 1)

                    count()
                    with pe.Fori(0, NCH) as i:
                        for fc, q, r in units:
                            pe.wait_ge(t_ready[q], START + 2 * i + r)
                            for k in range(KD):
                                ins = pe.matmul(psQ[q][:], wqk[:, k, fc * P:(fc + 1) * P], xT_all[:, bass.ds(i, 1), k * CH:(k + 1) * CH].rearrange("p c s -> p (c s)"),
                                                start=(k == 0), stop=(k == KD - 1))
                            ins.then_inc(q_in_psum[q], 1)

        def stage_experts():
            scope = ExitStack()
            with scope:
                listed_rows = sb("listed_rows", [NB, P], scope=scope)
                tokens = sb("tokens", [P, NB], I32, scope=scope)
                gidx = [sb(f"gidx{j}", [P, 1], I32, scope=scope) for j in range(2)]
                xg = [sb(f"xg{j}", [P, D], scope=scope) for j in range(2)]
                xgT = [sb(f"xgT{j}", [P, KD, P], scope=scope) for j in range(2)]
                w1_now = [sb(f"w1_now{j}", [P, KD, F], scope=scope) for j in range(2)]
                hT = [sb("hT0", [P, KF, P], scope=scope)[:], wqk[:].rearrange("p k (f t) -> p (k f) t", t=P)]
                y_sb = [wv[:, j, 0:D] for j in range(2)]
                psX = scope.enter_context(nc.psum_tensor("psX", [P, CH], F32))
                psH = [scope.enter_context(nc.psum_tensor(f"psH{j}", [P, KF, P], F32)) for j in range(2)]
                psY = [scope.enter_context(nc.psum_tensor(f"psY{j}", [P, CH], F32)) for j in range(2)]
                list_loaded, list_turned, tokens_ready = sem("list_loaded"), sem("list_turned"), sem("tokens_ready")
                gidx_ready, gathered = sems("gidx_ready"), pool_dma_sems("gathered")
                x_turned, xgT_ready = sem("x_turned"), sem("xgT_ready")
                w1_ready, h_in_psum, hT_ready = sem("w1_ready"), sem("h_in_psum"), sem("hT_ready")
                y_in_psum, y_ready, y_stored = sem("y_in_psum"), sem("y_ready"), sems("y_stored")
                block = scope.enter_context(nc.Block())
                NI = (NB - 1) // 2

                @block.sync
                def _(sp):
                    sp.dma_start(listed_rows[:], list_dram.rearrange("(b p) o -> b (p o)", p=P)).then_inc(list_loaded, 16)
                    with sp.Fori(0, NI) as i:
                        for j in (0, 1):
                            sp.wait_ge(y_ready, START + 2 * i + j + 1)
                            sp.dma_start(y_dram[bass.ds((2 * i + j) * P, P), :], y_sb[j]).then_inc(y_stored[j], 16)
                    sp.wait_ge(y_ready, START + NB)
                    sp.dma_start(y_dram[(NB - 1) * P:NB * P, :], y_sb[0]).then_inc(y_stored[0], 16)
                    sp.wait_ge(y_stored[0], START + 16 * NI + 16)
                    sp.wait_ge(y_stored[1], START + 16 * NI)

                @block.gpsimd
                def _(pool):
                    start_counts(pool)
                    pool.wait_ge(tokens_ready, START + 1)

                    def gather(i, j, first=False):
                        if not first:
                            pool.wait_ge(x_turned, START + 2 * i - 1 + j)
                            pool.wait_ge(gathered[j], 16 * i)
                        pool.tensor_copy(gidx[j][:], tokens[:, bass.ds(2 * i + j, 1)]).then_inc(gidx_ready[j], 1)
                        wait_apart(pool, "pool", gidx_ready[j], START + i + 1)
                        pool.indirect_dma_start(out=xg[j][:], out_offset=None, in_=xn_dram,
                                                in_offset=bass.IndirectOffsetOnAxis(ap=gidx[j][:, 0:1], axis=0),
                                                bounds_check=S - 1, oob_is_err=False).then_inc(gathered[j], 16)

                    gather(0, 0, first=True)
                    gather(0, 1, first=True)
                    with pool.Fori(1, NI) as i:
                        gather(i, 0)
                        gather(i, 1)
                    gather(NI, 0)

                @block.vector
                def _(dve):
                    def w1_copy(n, j, first=False):
                        expert = dve.value_load(expert_of[0:1, bass.ds(n, 1)], min_val=0, max_val=E - 1)
                        if not first:
                            dve.wait_ge(h_in_psum, START + n - 1)
                        dve.tensor_copy(w1_now[j][:], w1_sb[:, :, bass.ds(expert, 1), :].rearrange("p k e f -> p k (e f)")).then_inc(w1_ready, 1)

                    def x_copy(n, j, first=False):
                        dve.wait_ge(x_turned, START + n + 1)
                        if not first:
                            dve.wait_ge(h_in_psum, START + n - 1)
                        dve.tensor_copy(xgT[j][:], psX[:, 0:D].rearrange("p (k t) -> p k t", k=KD)).then_inc(xgT_ready, 1)

                    dve.wait_ge(w1_loaded, START + 16 * E)
                    w1_copy(0, 0, first=True)
                    w1_copy(1, 1, first=True)
                    dve.wait_ge(list_turned, START + 1)
                    dve.tensor_copy(tokens[:], psX[:, 0:NB]).then_inc(tokens_ready, 1)
                    x_copy(0, 0, first=True)
                    x_copy(1, 1, first=True)
                    with dve.Fori(1, NI) as i:
                        for j in (0, 1):
                            w1_copy(2 * i + j, j)
                            x_copy(2 * i + j, j)
                    w1_copy(NB - 1, 0)
                    x_copy(NB - 1, 0)

                @block.scalar
                def _(act):
                    def gelu(n, j):
                        act.wait_ge(h_in_psum, START + n + 1)
                        act.wait_ge(y_in_psum, START + n - 1 + CREDIT)
                        act.activation(hT[j], psH[j][:], ACT.Gelu).then_inc(hT_ready, 1)

                    def y_copy(n, i, j):
                        act.wait_ge(y_in_psum, START + n + 1 + CREDIT)
                        act.wait_ge(y_stored[j], START + 16 * i)
                        act.copy(y_sb[j], psY[j][:, 0:D]).then_inc(y_ready, 1)

                    gelu(0, 0)
                    with act.Fori(0, NI) as i:
                        for j in (0, 1):
                            gelu(2 * i + j + 1, 1 - j)
                            y_copy(2 * i + j, i, j)
                    y_copy(NB - 1, NI, 0)

                @block.tensor
                def _(pe):
                    pe.sem_inc(y_in_psum, CREDIT)
                    pe.wait_ge(list_loaded, START + 16)
                    pe.transpose(psX[:, 0:NB], listed_rows[:], ident[0:NB, 0:NB]).then_inc(list_turned, 1)
                    pe.wait_ge(tokens_ready, START + 1)

                    def turn_x(n, i, j):
                        pe.wait_ge(gathered[j], 16 * i + 16)
                        pe.wait_ge(xgT_ready, START + n)
                        for k in range(KD):
                            ins = pe.transpose(psX[:, k * P:(k + 1) * P], xg[j][:, k * P:(k + 1) * P], ident)
                        ins.then_inc(x_turned, 1)

                    def first(n, j, start=False):
                        pe.wait_ge(xgT_ready, START + n + 1)
                        pe.wait_ge(w1_ready, START + n + 1)
                        if not start:
                            pe.wait_ge(hT_ready, START + n - 1)
                        for c in range(KF):
                            for k in range(KD):
                                ins = pe.matmul(psH[j][:, c, :], w1_now[j][:, k, c * P:(c + 1) * P], xgT[j][:, k, :],
                                                start=(k == 0), stop=(k == KD - 1))
                        ins.then_inc(h_in_psum, 1)

                    def second(n, i, j):
                        expert = pe.value_load(expert_of[0:1, bass.ds(n, 1)], min_val=0, max_val=E - 1)
                        pe.wait_ge(hT_ready, START + n + 1)
                        pe.wait_ge(y_ready, START + 2 * i)
                        for k in range(KF):
                            ins = pe.matmul(psY[j][:, 0:D], hT[j][:, k, :],
                                            w2_sb[:, bass.ds(expert, 1), k, :].rearrange("p e d -> p (e d)"),
                                            start=(k == 0), stop=(k == KF - 1))
                        ins.then_inc(y_in_psum, 1)

                    turn_x(0, 0, 0)
                    turn_x(1, 0, 1)
                    first(0, 0, start=True)
                    first(1, 1, start=True)
                    turn_x(2, 1, 0)
                    pe.wait_ge(w2_loaded, START + 16 * E)
                    second(0, 0, 0)
                    first(2, 0)
                    turn_x(3, 1, 1)
                    second(1, 0, 1)
                    with pe.Fori(1, NI - 1) as i:
                        for j in (0, 1):
                            first(2 * i + j + 1, 1 - j)
                            turn_x(2 * i + j + 2, i + 1, j)
                            second(2 * i + j, i, j)
                    first(NB - 2, 1)
                    turn_x(NB - 1, NI, 0)
                    second(NB - 3, NI - 1, 0)
                    first(NB - 1, 0)
                    second(NB - 2, NI - 1, 1)
                    second(NB - 1, NI, 0)

        def stage_attend(attn, side):
            scope = ExitStack()
            with scope:
                qa = [sb(f"qa{j}", [AUG, S], BF16, scope=scope) for j in range(2)]
                ka = [sb(f"ka{j}", [AUG, S], BF16, scope=scope) for j in range(2)]
                vh = [sb(f"vh{j}", [P, NT, 32], scope=scope) for j in range(2)]
                probs = [sb(f"probs{j}", [P, 4, CH], scope=scope) for j in range(2)]
                oT = [sb(f"oT{j}", [P, CH], scope=scope) for j in range(2)]
                osum = sb("osum", [P, 4, VW], scope=scope)
                rden = sb("rden", [P, 4, 1], scope=scope)
                mxp = sb("mxp", [P, NT, NCH], scope=scope)
                nm = sb("nm", [P, HALF], scope=scope)
                nr = sb("nr", [P, HALF], scope=scope)
                nm3 = sb("nm3", [P, SPLIT, NT], BF16, scope=scope)
                mT = sb("mT", [SPLIT * NT, P], BF16, scope=scope)
                psS = scope.enter_context(nc.psum_tensor("psS", [P, RING, CH], F32))
                psM = scope.enter_context(nc.psum_tensor("psM", [P, RING, CH], F32))
                psO = scope.enter_context(nc.psum_tensor("psO", [P, CH], F32))
                psN = scope.enter_context(nc.psum_tensor("psN", [P, CH], F32))
                psMT = psN[:].bitcast(BF16)[0:SPLIT * NT, CH:CH + P]
                aug_ones, pads = sem("aug_ones"), sem("pads")
                loaded, late_half_loaded = sems("loaded"), sem("late_half_loaded")
                v_ready = sem("v_ready")
                s_ready, exp_done, pv_done = sem("s_ready"), sem("exp_done"), sem("pv_done")
                o_copied, o_turned, o_summed = sem("o_copied"), sem("o_turned"), sem("o_summed")
                recip, normed = sem("recip"), sem("normed")
                m_ready, m_done, m_chain = sem("m_ready"), sem("m_done"), sem("m_chain")
                negm_ready, negm_turned, negm_copied, negm_loaded = (
                    sem("negm_ready"), sem("negm_turned"), sem("negm_copied"), sem("negm_loaded"))
                yg = [sb(f"yg{k}", [P, D], scope=scope) for k in range(TOPK)]
                xr = sb("xr", [P, D], scope=scope)
                yidx = [sb(f"yidx{k}", [P, 1], I32, scope=scope) for k in range(TOPK)]
                ygate = [sb(f"ygate{k}", [P, 1], scope=scope) for k in range(TOPK)]
                (y_here, xr_here), side_step = pool_dma_sems("side_rows"), sem("side_step")
                SIDE_STEPS = 9
                M_LINKS = 5
                FIRST_LOAD, LOAD = 16 * 2 * SPLIT, 16 * 2 * SPLIT * 4
                TURN_EARLY, TURN_LATE = EARLY_OVER + 2, LATE_OVER + 2
                assert 3 <= TURN_EARLY < TURN_LATE < NQ - 1 and QUADS[TURN_EARLY + 2][0] > NCH // 2
                block = scope.enter_context(nc.Block())

                FIRST_TURN = len(TILES_LATE) + M_LINKS + 1
                assert FIRST_TURN + 2 < len(FIRST_TILES)

                def heads(eng, step):
                    NI = H // 2 - 1
                    with eng.Fori(0, NI) as i:
                        step(2 * i, 0, i)
                        step(2 * i + 1, 1, i)
                    step(H - 2, 0, NI, last=True)
                    step(H - 1, 1, NI, last=True)

                def passes(eng, step):
                    step(0, 0, 1, 0)
                    with eng.Fori(0, H // 2 - 1) as i:
                        step(2 * i + 1, 1, 2 * i + 2, i + 1)
                        step(2 * i + 2, 0, 2 * i + 3, i + 1)
                    step(H - 1, 1, None, None)

                def tiles_of(u, g):
                    return [(t, t >= LATE_AT) for t in BESIDE[u] if g is not None or t < LATE_AT]

                def back(h, j, u, quads):
                    if u >= quads:
                        return h, j, u - quads
                    return None if isinstance(h, int) and h == 0 else (h - 1, 1 - j, u - quads + NQ)

                def places(u):
                    qt, b = QUADS[u]
                    if b < qt or qt == 0:
                        return [(g, 0, CH) for g in range(4)]
                    return [(0, 0, CH), (1, 0, 3 * P), (2, 0, 2 * P), (2, 2 * P, P)]

                widths = [[sum(w for n, _, w in places(u) if n == m) for m in range(places(u)[3][0] + 1)] for u in range(NQ)]
                first_unit = [sum(len(w) for w in widths[:u]) for u in range(NQ + 1)]
                NU = first_unit[NQ]

                def before(n):
                    return n - RING if n >= RING else max(m for m in range(NU) if m % RING == n) - NU

                @block.sync
                def _(sp):
                    def load(g, j, cols, arrived):
                        f = bass.ds(g * HD, HD)
                        r = 0
                        for which in range(SPLIT):
                            n = SPLIT - which
                            sp.dma_start(qa[j][r:r + n * HD, cols], qk_dram[0, 0:n, f, cols]).then_inc(arrived, 16)
                            sp.dma_start(ka[j][r:r + n * HD, cols],
                                         qk_dram[1, which:which + 1, f, cols].to_broadcast([n, HD, cols.stop - cols.start])).then_inc(arrived, 16)
                            r += n * HD

                    def negm(j, n, late):
                        sp.wait_ge(negm_copied, START + n + 1)
                        cols = slice(S // 2, S) if late else slice(0, S // 2)
                        for c in range(SPLIT):
                            sp.dma_start(qa[j][PAIRS * HD + c:PAIRS * HD + c + 1, cols].rearrange("c (b q) -> c b q", q=P),
                                         mT[c * NT + late * HALF:c * NT + (late + 1) * HALF, :]).then_inc(negm_loaded, 16)

                    load(0, 0, slice(S // 2, S), late_half_loaded)
                    load(0, 0, slice(0, S // 2), loaded[0])
                    load(1, 1, slice(0, S), loaded[1])
                    negm(0, 0, late=True)

                    def step(h, j, i, last=False):
                        for part in range(4):
                            if part == 0:
                                negm(j, 2 * h + 1, late=False)
                            if part == 2 and not (isinstance(h, int) and h == H - 1):
                                negm(1 - j, 2 * h + 2, late=True)
                            if not last:
                                done = max(u for u in range(NQ) if QUADS[u][0] == 6 - 2 * part)
                                wait_apart(sp, "sp", pv_done, START + NQ * h + done + 1 + CREDIT)
                                load(h + 2, j, slice((3 - part) * 2 * CH, (4 - part) * 2 * CH), loaded[j])

                    heads(sp, step)

                @block.gpsimd
                def _(pool):
                    start_counts(pool)
                    for j in (0, 1):
                        pool.memset(ka[j][PAIRS * HD:AUG, :], 1.0).then_inc(aug_ones, 1)
                    pool.wait_ge(aug_ones, START + 2)
                    for j in (0, 1):
                        pool.memset(vh[j][:, :, VW:32], 0.0).then_inc(pads, 1)
                    pool.wait_ge(pads, START + 2)
                    for g in (0, 1):
                        pool.tensor_copy(vh[g][:, :, 0:VW], v_all[:, g]).then_inc(v_ready, 1)

                    def side_sum(n):
                        at_step = [0]

                        def after(ins, k=1):
                            ins.then_inc(side_step, 1)
                            at_step[0] += 1
                            wait_apart(pool, "pool", side_step, START + SIDE_STEPS * n + at_step[0])

                        cols = bass.ds(n, 1)
                        pool.dma_start(xr[:], x_rows[bass.ds(n * P, P), :]).then_inc(xr_here, 16)
                        for k in range(TOPK):
                            after(pool.tensor_copy(yidx[k][:], slot_in[:, k, cols]))
                            after(pool.tensor_copy(ygate[k][:], gates[:, k, cols]))
                            pool.indirect_dma_start(out=yg[k][:], out_offset=None, in_=y_dram,
                                                    in_offset=bass.IndirectOffsetOnAxis(ap=yidx[k][:, 0:1], axis=0),
                                                    bounds_check=NB * P - 1, oob_is_err=False).then_inc(y_here, 16)
                        wait_apart(pool, "pool", xr_here, 16 * n + 16)
                        after(pool.tensor_tensor(xr[:], xr[:], bp[:], ALU.add))
                        wait_apart(pool, "pool", y_here, 32 * n + 32)
                        for k in range(TOPK):
                            after(pool.tensor_scalar(yg[k][:], yg[k][:], ygate[k][:, 0:1], None, ALU.mult))
                        after(pool.tensor_tensor(yg[0][:], yg[0][:], xr[:], ALU.add))
                        after(pool.tensor_tensor(side[:, cols, :].rearrange("p b d -> p (b d)"), yg[0][:], yg[1][:], ALU.add))
                        assert at_step[0] == SIDE_STEPS

                    def step(h, j, i, last=False):
                        side_sum(2 * h)
                        side_sum(2 * h + 1)
                        if not last:
                            pool.wait_ge(pv_done, START + NQ * h + NQ + CREDIT)
                            pool.tensor_copy(vh[j][:, :, 0:VW], v_all[:, bass.ds(h + 2, 1)].rearrange("p h b d -> p (h b) d")).then_inc(v_ready, 1)

                    heads(pool, step)

                @block.vector
                def _(dve):
                    dve.memset(nm3[:], 0.0)
                    dve.memset(mxp[:], -3.0e38).then_inc(m_chain, 1)
                    dve.wait_ge(m_chain, START + 1)
                    dve.sem_inc(m_done, RING)

                    def tile(n, k, tile):
                        i, c = tile
                        dve.wait_ge(m_ready, START + n + 1)
                        dve.tensor_reduce(mxp[:, i, c:c + 1], psM[:, k % RING, 0:tile_width(tile)], AX, ALU.max).then_inc(m_done, 1)

                    def finish(n, late, tiles, part):
                        rows = slice(HALF, NT) if late else slice(0, HALF)
                        dve.wait_ge(m_chain, START + M_LINKS * n + part + 1)
                        if part == 0:
                            dve.wait_ge(m_done, START + tiles + RING)
                            ins = dve.tensor_reduce(nm[:], mxp[:, rows, :], AX, ALU.max)
                        if part == 1:
                            dve.wait_ge(negm_turned, START + n)
                            ins = dve.tensor_scalar(nm3[:, 0, rows], nm[:], -1.0, None, ALU.mult)
                        if part == 2:
                            ins = dve.scalar_tensor_tensor(out=nr[:], in0=nm[:], scalar=-1.0, in1=nm3[:, 0, rows],
                                                           op0=ALU.mult, op1=ALU.subtract)
                        if part == 3:
                            ins = dve.tensor_copy(nm3[:, 1, rows], nr[:])
                        if part == 4:
                            ins = dve.tensor_tensor(nm3[:, 2, rows], nr[:], nm3[:, 1, rows], ALU.subtract)
                        ins.then_inc(m_chain, 1)

                    def keep_negm(n):
                        dve.wait_ge(negm_turned, START + n + 1)
                        dve.wait_ge(negm_loaded, START + 16 * SPLIT * n)
                        dve.tensor_copy(mT[:], psMT).then_inc(negm_copied, 1)

                    def normalize(h, u, part):
                        qt = QUADS[u][0]
                        q = NCH * h + NCH - 1 - qt
                        if part == 0:
                            dve.wait_ge(o_turned, START + q + 1 + CREDIT)
                            dve.wait_ge(normed, START + q)
                            groups = psN[:].rearrange("p (b g d) -> p b d g", b=4, g=4)
                            dve.tensor_reduce(osum[:], groups[:, :, 0:VW, :], AX, ALU.add).then_inc(o_summed, 1)
                        if part == 1:
                            dve.wait_ge(o_summed, START + q + 1)
                            dve.reciprocal(rden[:], osum[:, :, HD:VW]).then_inc(recip, 1)
                        if part == 2:
                            dve.wait_ge(recip, START + q + 1)
                            dve.tensor_tensor(attn[:, 4 * qt:4 * qt + 4, bass.ds(h * HD, HD)], osum[:, :, 0:HD],
                                              rden[:].to_broadcast([P, 4, HD]), ALU.mult).then_inc(normed, 1)

                    for t, at_tile in enumerate(FIRST_TILES):
                        tile(t, t, at_tile)
                        part = t - len(TILES_LATE)
                        if 0 <= part < M_LINKS:
                            finish(0, True, len(TILES_LATE), part)
                        if t == FIRST_TURN + 2:
                            keep_negm(0)

                    def step(h, j, g, i):
                        before_head = NTL * h + len(FIRST_TILES)
                        for u in range(NQ):
                            tiles = tiles_of(u, g)
                            done = before_head + (BESIDE[u].start if g is not None else min(BESIDE[u].start, LATE_AT))
                            ended = back(h, j, u, 3)
                            for n in range(max(len(tiles), M_LINKS)):
                                if n < len(tiles):
                                    t, _ = tiles[n]
                                    tile(before_head + t, len(FIRST_TILES) + t, STREAM[t])
                                if n < 3 and ended and ends_tile(ended[2]):
                                    normalize(ended[0], ended[2], n)
                                if n < M_LINKS and u == EARLY_OVER + 1:
                                    finish(2 * h + 1, False, done, n)
                                if n < M_LINKS and u == LATE_OVER + 1 and g is not None:
                                    finish(2 * h + 2, True, done, n)
                                if n == 0 and u == TURN_EARLY + 1:
                                    keep_negm(2 * h + 1)
                                if n == 0 and u == TURN_LATE + 1 and g is not None:
                                    keep_negm(2 * h + 2)

                    passes(dve, step)
                    for u in (NQ - 3, NQ - 2, NQ - 1):
                        if ends_tile(u):
                            for part in range(3):
                                normalize(H - 1, u, part)

                @block.scalar
                def _(act):
                    act.sem_inc(exp_done, RING)

                    def exps(h, u):
                        for m, w in enumerate(widths[u]):
                            n = first_unit[u] + m
                            act.wait_ge(s_ready, START + NU * h + n + 1)
                            if m == 0:
                                act.wait_ge(pv_done, START + NQ * h + u + 1)
                            act.activation(probs[u % 2][:, m, 0:w], psS[:, n % RING, 0:w], ACT.Exp).then_inc(exp_done, 1)

                    def o_copy(h, u):
                        q = NCH * h + NCH - 1 - QUADS[u][0]
                        act.wait_ge(pv_done, START + NQ * h + u + 1 + CREDIT)
                        act.wait_ge(o_turned, START + q + 1)
                        act.copy(oT[(NCH - 1 - QUADS[u][0]) % 2][:], psO[:]).then_inc(o_copied, 1)

                    def step(h, j, g, i):
                        for u in range(NQ):
                            exps(h, u)
                            last = back(h, j, u, 1)
                            if last and ends_tile(last[2]):
                                o_copy(last[0], last[2])

                    passes(act, step)
                    o_copy(H - 1, NQ - 1)

                @block.tensor
                def _(pe):
                    pe.sem_inc(pv_done, CREDIT)
                    pe.sem_inc(o_turned, CREDIT)
                    pe.wait_ge(aug_ones, START + 2)
                    pe.wait_ge(pads, START + 2)

                    def tile(n, k, jg, tile):
                        i, c = tile
                        w = tile_width(tile)
                        diagonal = c == i // 4
                        pe.wait_ge(m_done, START + n + 1)
                        ins = pe.matmul(psM[:, k % RING, 0:w], qa[jg][0:PAIRS * HD, i * P:(i + 1) * P], ka[jg][0:PAIRS * HD, c * CH:c * CH + w],
                                        start=True, stop=not diagonal)
                        if diagonal:
                            ins = pe.matmul(psM[:, k % RING, w - P:w], identb[:], maskS[:], start=False, stop=True)
                        ins.then_inc(m_ready, 1)

                    def scores(h, j, u, g):
                        qt, b = QUADS[u]
                        m, col, w = places(u)[g]
                        n = first_unit[u] + m
                        kb = 4 * b + g
                        if col == 0:
                            pe.wait_ge(exp_done, START + NU * h + before(n) + 1 + RING)
                        out_at = psS[:, n % RING, :]
                        ins = pe.matmul(out_at[:, col:col + w], ka[j][:, kb * P:(kb + 1) * P],
                                        qa[j][:, (qt + 1) * CH - w:(qt + 1) * CH], start=True, stop=b < qt)
                        if b == qt:
                            m = P if w < CH or g == 0 else (g + 1) * P
                            ins = pe.matmul(out_at[:, col:col + m], identb[:], maskT[:, 4 * P - m:4 * P], start=False, stop=True)
                        if col + w == widths[u][places(u)[g][0]]:
                            ins.then_inc(s_ready, 1)

                    def products(h, j, u):
                        qt, b = QUADS[u]
                        pe.wait_ge(exp_done, START + NU * h + first_unit[u + 1] + RING)
                        if b == 0:
                            pe.wait_ge(o_copied, START + NCH * h + NCH - 1 - qt)
                        pieces = DIAGONAL if b == qt and qt > 0 else WHOLE
                        for n, (kb, group, lo, hi) in enumerate(pieces):
                            over = b == qt and group not in [piece[1] for piece in pieces[n + 1:]]
                            m, col, w = places(u)[kb]
                            at = col + lo - (CH - w)
                            ins = pe.matmul(psO[32 * group:32 * group + 32, lo:hi], vh[j][:, 4 * b + kb, :],
                                            probs[u % 2][:, m, at:at + hi - lo], start=(b == 0), stop=over,
                                            tile_position=(0, 32 * group))
                        ins.then_inc(pv_done, 1)

                    def turn(h, u, maxima=None):
                        qt = QUADS[u][0]
                        q = NCH * h + NCH - 1 - qt
                        pe.wait_ge(o_copied, START + q + 1)
                        pe.wait_ge(o_summed, START + q)
                        if maxima is not None:
                            pe.wait_ge(negm_copied, START + maxima + 1)
                        for b in range(4):
                            ins = pe.transpose(psN[:, b * P:(b + 1) * P], oT[(NCH - 1 - qt) % 2][:, b * P:(b + 1) * P], ident)
                        ins.then_inc(o_turned, 1)

                    def turn_negm(n, turned):
                        pe.wait_ge(m_chain, START + M_LINKS * n + M_LINKS + 1)
                        pe.wait_ge(o_summed, START + turned)
                        pe.transpose(psMT, nm3[:].rearrange("p c b -> p (c b)"), identb[:]).then_inc(negm_turned, 1)

                    pe.wait_ge(late_half_loaded, START + FIRST_LOAD)
                    for t, at_tile in enumerate(FIRST_TILES):
                        if at_tile == (HALF, NCH // 2 - 1):
                            pe.wait_ge(loaded[0], START + FIRST_LOAD)
                        tile(t, t, 0, at_tile)
                        if t == FIRST_TURN:
                            turn_negm(0, 0)

                    def step(h, j, g, i):
                        maxima = None
                        turned = NCH * h
                        for u in range(NQ):
                            tiles = tiles_of(u, g)
                            for n in range(4):
                                for t, of_next in tiles[n * len(tiles) // 4:(n + 1) * len(tiles) // 4]:
                                    if t == LATE_AT:
                                        pe.wait_ge(loaded[1 - j], START + FIRST_LOAD + LOAD * i)
                                    tile(NTL * h + len(FIRST_TILES) + t, len(FIRST_TILES) + t, 1 - j if of_next else j, STREAM[t])
                                if u == 0 and n == 0:
                                    pe.wait_ge(negm_loaded, START + 16 * SPLIT * (2 * h + 1))
                                    pe.wait_ge(v_ready, START + h + 1)
                                if QUADS[u] == (NCH // 2 - 1, 0) and n == 0:
                                    pe.wait_ge(negm_loaded, START + 16 * SPLIT * (2 * h + 2))
                                scores(h, j, u, n)
                            last, before_last = back(h, j, u, 1), back(h, j, u, 2)
                            if last:
                                products(*last)
                            if u == TURN_EARLY:
                                maxima = 2 * h + 1
                                turn_negm(maxima, turned)
                            if u == TURN_LATE and g is not None:
                                maxima = 2 * h + 2
                                turn_negm(maxima, turned)
                            if before_last and ends_tile(before_last[2]):
                                turn(before_last[0], before_last[2], maxima)
                                maxima = None
                                turned = turned + 1 if u >= 2 else turned

                    passes(pe, step)
                    products(H - 1, 1, NQ - 1)
                    for u in (NQ - 2, NQ - 1):
                        turn(H - 1, u)

        def stage_output(attn, side):
            scope = ExitStack()
            with scope:
                at_st = [sb(f"at_st{j}", [P, D], scope=scope) for j in range(2)]
                aT = [sb(f"aT{j}", [P, KD, P], scope=scope) for j in range(2)]
                res = [sb(f"res{j}", [P, D], scope=scope) for j in range(2)]
                psA = [scope.enter_context(nc.psum_tensor(f"psA{j}", [P, CH], F32)) for j in range(2)]
                psP = [scope.enter_context(nc.psum_tensor(f"psP{j}", [P, CH], F32)) for j in range(2)]
                staged = sems("staged")
                a_turned, aT_ready, projected = sems("a_turned"), sems("aT_ready"), sems("projected")
                res_ready, res_stored = sems("res_ready"), sems("res_stored")
                block = scope.enter_context(nc.Block())
                NI = NT // 2

                @block.sync
                def _(sp):
                    with sp.Fori(0, NI) as i:
                        for j in (0, 1):
                            sp.wait_ge(res_ready[j], START + i + 1)
                            sp.dma_start(out_rows[bass.ds((2 * i + j) * P, P), :], res[j][:]).then_inc(res_stored[j], 16)
                    for j in (0, 1):
                        sp.wait_ge(res_stored[j], START + 16 * NI)

                @block.gpsimd
                def _(pool):
                    start_counts(pool)

                @block.scalar
                def _(act):
                    with act.Fori(0, NI) as i:
                        for j in (0, 1):
                            act.wait_ge(a_turned[j], START + i + 1)
                            act.wait_ge(projected[j], START + i)
                            act.copy(aT[j][:], psA[j][:, 0:D].rearrange("p (k t) -> p k t", k=KD)).then_inc(aT_ready[j], 1)

                @block.vector
                def _(dve):
                    def stage(i, j, first=False):
                        if not first:
                            dve.wait_ge(a_turned[j], START + i)
                        dve.tensor_copy(at_st[j][:], attn[:, bass.ds(2 * i + j, 1), :].rearrange("p b d -> p (b d)")).then_inc(staged[j], 1)

                    def finish(i, j):
                        dve.wait_ge(projected[j], START + i + 1)
                        dve.wait_ge(res_stored[j], START + 16 * i)
                        dve.tensor_tensor(res[j][:], psP[j][:, 0:D], side[:, bass.ds(2 * i + j, 1), :].rearrange("p b d -> p (b d)"),
                                          ALU.add).then_inc(res_ready[j], 1)

                    stage(0, 0, first=True)
                    stage(0, 1, first=True)
                    with dve.Fori(0, NI - 1) as i:
                        for j in (0, 1):
                            stage(i + 1, j)
                            finish(i, j)
                    finish(NI - 1, 0)
                    finish(NI - 1, 1)

                @block.tensor
                def _(pe):
                    def turn(i, j):
                        pe.wait_ge(staged[j], START + i + 1)
                        pe.wait_ge(aT_ready[j], START + i)
                        for k in range(KD):
                            ins = pe.transpose(psA[j][:, k * P:(k + 1) * P], at_st[j][:, k * P:(k + 1) * P], ident)
                        ins.then_inc(a_turned[j], 1)

                    def project(i, j):
                        pe.wait_ge(aT_ready[j], START + i + 1)
                        pe.wait_ge(res_ready[j], START + i)
                        for k in range(KD):
                            ins = pe.matmul(psP[j][:, 0:D], aT[j][:, k, :], wp[:, k, :], start=(k == 0), stop=(k == KD - 1))
                        ins.then_inc(projected[j], 1)

                    turn(0, 0)
                    with pe.Fori(0, NI - 1) as i:
                        turn(i, 1)
                        project(i, 0)
                        turn(i + 1, 0)
                        project(i, 1)
                    turn(NI - 1, 1)
                    project(NI - 1, 0)
                    project(NI - 1, 1)

        stage_tokens()
        stage_queries()
        stage_experts()
        weights.close()
        attn, side = sb("attn", [P, NT, D]), sb("side", [P, NT, D])
        stage_attend(attn, side)
        stage_output(attn, side)


def kernel(L0_attn_hidden_states, L0_attn_c_attn_w, L0_attn_c_attn_b, L0_attn_c_proj_w, L0_attn_c_proj_b,
           L0_ffn_router_w, L0_ffn_w1, L0_ffn_w2):
    import concourse.bacc as bacc
    from concourse.bass_utils import run_bass_kernel_spmd

    nc = bacc.Bacc("TRN2", target_bir_lowering=False, num_devices=1)
    arrays = {
        "x": L0_attn_hidden_states, "w_attn": L0_attn_c_attn_w, "b_attn": np.asarray(L0_attn_c_attn_b)[None, :],
        "b_qk": np.asarray(L0_attn_c_attn_b)[:2 * D].reshape(4, P).T, "w_proj": L0_attn_c_proj_w, "b_proj": np.asarray(L0_attn_c_proj_b)[None, :],
        "w_router": np.asarray(L0_ffn_router_w).T, "w1": L0_ffn_w1, "w2": L0_ffn_w2, "consts": const_array(),
    }
    arrays = {n: np.ascontiguousarray(a) for n, a in arrays.items()}
    args = [nc.dram_tensor(n, a.shape, mybir.dt.from_np(a.dtype), kind="ExternalInput").ap() for n, a in arrays.items()]
    out = nc.dram_tensor("out", (1, S, D), F32, kind="ExternalOutput").ap()
    build(nc, *args, out)
    r = run_bass_kernel_spmd(nc, [arrays], core_ids=[0])
    return r.results[0]["out"]
```
